# Optimizing a Trainium2 kernel written in Bass

```python
import numpy as np
import jax
import jax.numpy as jnp

def _softmax(x, axis=-1):
    return jax.nn.softmax(x, axis=axis)

def _gelu(x):
    return jax.nn.gelu(x, approximate=True)

def _silu(x):
    return jax.nn.silu(x)

def _sigmoid(x):
    return jax.nn.sigmoid(x)

def _layernorm(x, axis=-1, eps=1e-05):
    m = jnp.mean(x, axis=axis, keepdims=True)
    v = jnp.var(x, axis=axis, keepdims=True)
    return (x - m) / jnp.sqrt(v + eps)

def _scatter_add(tgt, idx, src, axis=0):
    return tgt.at[idx].add(src)

def _segment_sum(src, seg, n):
    return jax.ops.segment_sum(src, seg, n)
kernel_name = 'mk_cond_resid_d1_seqx_r4_55f2ae'

def setup_inputs(seed: int=0):
    np.random.seed(seed)
    _w = jnp.asarray

    def _rec_inputs():
        import jax
        import jax.numpy as jnp
        _rk = jax.random.key(seed)
        x = 7.22e-05 + 1 * jax.random.normal(jax.random.fold_in(_rk, 1), (128, 64, 256), jnp.float32)
        _lenS = 64 - jax.random.randint(jax.random.fold_in(_rk, 7), (128,), 0, max(1, 64 // 4) + 1, jnp.int32)
        _lenS2 = 64 - jax.random.randint(jax.random.fold_in(_rk, 8), (128,), 0, max(1, 64 // 4) + 1, jnp.int32)
        cond_256 = 0.000887014 + 1.03683 * jax.random.normal(jax.random.fold_in(_rk, 11), (128, 64), jnp.float32)
        return (x, cond_256)
    x, cond_256 = _rec_inputs()

    def _L0_cond_setup():
        import jax, jax.numpy as jnp
        import numpy as np
        D_MODEL = 256
        D_T = 64
        N_HEADS = 16
        HIDDEN = 4 * D_MODEL
        EPS = 1e-06

        def _tc_rmsnorm(x, t, gw, gb, bw, bb):
            g = (t @ gw.T + gb)[:, None, :]
            b = (t @ bw.T + bb)[:, None, :]
            inv_rms = jax.lax.rsqrt(jnp.mean(x * x, axis=-1, keepdims=True) + EPS)
            return g * x * inv_rms + b

        def _attention(x, Wq, Wk, Wv, Wo):
            B, L, D = x.shape
            H = N_HEADS
            dh = D // H
            scale = np.sqrt(dh).astype(np.float32)
            q = (x @ Wq.T).reshape(B, L, H, dh)
            k = (x @ Wk.T).reshape(B, L, H, dh)
            v = (x @ Wv.T).reshape(B, L, H, dh)
            attn = jnp.einsum('blhd,bmhd->bhlm', q, k) / scale
            p = jax.nn.softmax(attn, axis=-1)
            o = jnp.einsum('bhlm,bmhd->blhd', p, v).reshape(B, L, D)
            return o @ Wo.T

        def _swiglu(x, gate_w, hid_w, out_w):
            return jax.nn.silu(x @ gate_w.T) * (x @ hid_w.T) @ out_w.T
        key = jax.random.key(seed)
        ks = jax.random.split(key, 20)
        B, L = (8, 256)
        s_d = 1.0 / np.sqrt(D_MODEL)
        s_t = 1.0 / np.sqrt(D_T)
        s_h = 1.0 / np.sqrt(HIDDEN)
        return {'x': jax.random.normal(ks[0], (B, L, D_MODEL), jnp.float32), 't': jax.random.normal(ks[1], (B, D_T), jnp.float32), 'Wq': jax.random.normal(ks[2], (D_MODEL, D_MODEL), jnp.float32) * s_d, 'Wk': jax.random.normal(ks[3], (D_MODEL, D_MODEL), jnp.float32) * s_d, 'Wv': jax.random.normal(ks[4], (D_MODEL, D_MODEL), jnp.float32) * s_d, 'Wo': jax.random.normal(ks[5], (D_MODEL, D_MODEL), jnp.float32) * s_d, 'g1w': jax.random.normal(ks[6], (D_MODEL, D_T), jnp.float32) * s_t, 'g1b': jnp.ones((D_MODEL,), jnp.float32), 'b1w': jax.random.normal(ks[7], (D_MODEL, D_T), jnp.float32) * s_t, 'b1b': jnp.zeros((D_MODEL,), jnp.float32), 'g2w': jax.random.normal(ks[8], (D_MODEL, D_T), jnp.float32) * s_t, 'g2b': jnp.ones((D_MODEL,), jnp.float32), 'b2w': jax.random.normal(ks[9], (D_MODEL, D_T), jnp.float32) * s_t, 'b2b': jnp.zeros((D_MODEL,), jnp.float32), 'gate_w': jax.random.normal(ks[10], (HIDDEN, D_MODEL), jnp.float32) * s_d, 'hid_w': jax.random.normal(ks[11], (HIDDEN, D_MODEL), jnp.float32) * s_d, 'out_w': jax.random.normal(ks[12], (D_MODEL, HIDDEN), jnp.float32) * s_h}
    _L0_cond_all = _L0_cond_setup()
    _L0_cond_in = {k: v for k, v in _L0_cond_all.items() if k in ('Wq', 'Wk', 'Wv', 'Wo', 'g1w', 'g1b', 'b1w', 'b1b', 'g2w', 'g2b', 'b2w', 'b2b', 'gate_w', 'hid_w', 'out_w')}
    del _L0_cond_all
    return {'x': x, 'cond_256': cond_256, 'L0_cond_Wq': _L0_cond_in['Wq'], 'L0_cond_Wk': _L0_cond_in['Wk'], 'L0_cond_Wv': _L0_cond_in['Wv'], 'L0_cond_Wo': _L0_cond_in['Wo'], 'L0_cond_g1w': _L0_cond_in['g1w'], 'L0_cond_g1b': _L0_cond_in['g1b'], 'L0_cond_b1w': _L0_cond_in['b1w'], 'L0_cond_b1b': _L0_cond_in['b1b'], 'L0_cond_g2w': _L0_cond_in['g2w'], 'L0_cond_g2b': _L0_cond_in['g2b'], 'L0_cond_b2w': _L0_cond_in['b2w'], 'L0_cond_b2b': _L0_cond_in['b2b'], 'L0_cond_gate_w': _L0_cond_in['gate_w'], 'L0_cond_hid_w': _L0_cond_in['hid_w'], 'L0_cond_out_w': _L0_cond_in['out_w']}

def reference(x, cond_256, L0_cond_Wq, L0_cond_Wk, L0_cond_Wv, L0_cond_Wo, L0_cond_g1w, L0_cond_g1b, L0_cond_b1w, L0_cond_b1b, L0_cond_g2w, L0_cond_g2b, L0_cond_b2w, L0_cond_b2b, L0_cond_gate_w, L0_cond_hid_w, L0_cond_out_w):
    import jax
    import jax.numpy as jnp

    def _L0_cond_ref(x, t, Wq, Wk, Wv, Wo, g1w, g1b, b1w, b1b, g2w, g2b, b2w, b2b, gate_w, hid_w, out_w):
        import jax, jax.numpy as jnp
        import numpy as np
        D_MODEL = 256
        D_T = 64
        N_HEADS = 16
        HIDDEN = 4 * D_MODEL
        EPS = 1e-06

        def _tc_rmsnorm(x, t, gw, gb, bw, bb):
            g = (t @ gw.T + gb)[:, None, :]
            b = (t @ bw.T + bb)[:, None, :]
            inv_rms = jax.lax.rsqrt(jnp.mean(x * x, axis=-1, keepdims=True) + EPS)
            return g * x * inv_rms + b

        def _attention(x, Wq, Wk, Wv, Wo):
            B, L, D = x.shape
            H = N_HEADS
            dh = D // H
            scale = np.sqrt(dh).astype(np.float32)
            q = (x @ Wq.T).reshape(B, L, H, dh)
            k = (x @ Wk.T).reshape(B, L, H, dh)
            v = (x @ Wv.T).reshape(B, L, H, dh)
            attn = jnp.einsum('blhd,bmhd->bhlm', q, k) / scale
            p = jax.nn.softmax(attn, axis=-1)
            o = jnp.einsum('bhlm,bmhd->blhd', p, v).reshape(B, L, D)
            return o @ Wo.T

        def _swiglu(x, gate_w, hid_w, out_w):
            return jax.nn.silu(x @ gate_w.T) * (x @ hid_w.T) @ out_w.T
        x = x + _attention(_tc_rmsnorm(x, t, g1w, g1b, b1w, b1b), Wq, Wk, Wv, Wo)
        return x + _swiglu(_tc_rmsnorm(x, t, g2w, g2b, b2w, b2b), gate_w, hid_w, out_w)
    x = x + _L0_cond_ref(x, cond_256, L0_cond_Wq, L0_cond_Wk, L0_cond_Wv, L0_cond_Wo, L0_cond_g1w, L0_cond_g1b, L0_cond_b1w, L0_cond_b1b, L0_cond_g2w, L0_cond_g2b, L0_cond_b2w, L0_cond_b2b, L0_cond_gate_w, L0_cond_hid_w, L0_cond_out_w)
    return x

_drawn_inputs = setup_inputs


def setup_inputs(seed=0):
    import zlib

    import numpy as np

    out = dict(_drawn_inputs(seed))
    spreads = {'L0_cond_g1b': (1.0, 0.2),
     'L0_cond_b1b': (0.0, 0.1),
     'L0_cond_g2b': (1.0, 0.2),
     'L0_cond_b2b': (0.0, 0.1)}
    factors = {}
    for name, (base, spread) in spreads.items():
        noise = np.random.default_rng([zlib.crc32(name.encode()), seed]).standard_normal(out[name].shape)
        drawn = base * np.exp(spread * noise) if base else spread * noise
        out[name] = jnp.asarray(drawn.astype(out[name].dtype))
    for name, factor in factors.items():
        out[name] = (out[name] * factor).astype(out[name].dtype)
    return out
```

```python
from contextlib import ExitStack

import concourse.bass as bass
from concourse import mybir

ALU = mybir.AluOpType
ACT = mybir.ActivationFunctionType
AX_X = mybir.AxisListType.X
F32 = mybir.dt.float32
F32R = mybir.dt.float32r

P = 128
B, L, D = 128, 64, 256
DT = 64
HEADS, DH = 16, 16
HID = 4 * D
EPS = 1e-6
SEQS = 8
TOK = SEQS * L
TILES = B // SEQS
BLK = TOK // P
CH = D // P
PAIRS = HEADS // 2
ROWS = 2 * DH
CHUNKS = HID // P
VW = 2 * ROWS + 2

GATE, HIDDEN, Y, SCORE, TRANS, OUT, EXTRA = 0, 1, 2, 4, 5, 6, 7


def conditioned_block(nc, x, condT, WqT, WkT, WvT, WoT, g1wT, g1b, b1wT, b1b, g2wT, g2b, b2wT, b2b,
                      gateT, hidT, outT, consts, out):
    x_t = x.rearrange("(t k s) l c -> t (s l) k c", k=BLK, s=P // L)
    out_t = out.rearrange("(t k s) l c -> t (s l) k c", k=BLK, s=P // L)

    with ExitStack() as ctx:
        def sb(name, shape, dt=F32):
            return ctx.enter_context(nc.sbuf_tensor(name, shape, dt))

        def sem(name):
            return ctx.enter_context(nc.semaphore(name))

        ps = ctx.enter_context(nc.psum_tensor("ps", [P, 8, 512], F32))

        ident_mask = sb("ident_mask", [P, P + 2])
        ident = ident_mask[:, 0:P]
        raw = sb("raw", [P, 2, 2048])
        att_w_hi = sb("att_w_hi", [P, 4, CH, D], F32R)
        att_w_lo = sb("att_w_lo", [P, 4, CH, D], F32R)
        gate_w_hi = sb("gate_w_hi", [P, CH, HID], F32R)
        gate_w_lo = sb("gate_w_lo", [P, CH, HID], F32R)
        hid_w_hi = sb("hid_w_hi", [P, CH, HID], F32R)
        hid_w_lo = sb("hid_w_lo", [P, CH, HID], F32R)
        out_w_hi = sb("out_w_hi", [P, CHUNKS, D], F32R)
        out_w_lo = sb("out_w_lo", [P, CHUNKS, D], F32R)
        cond_sb = sb("cond_sb", [DT, B])
        mod_w = sb("mod_w", [DT, 4, D])
        mod_bias = sb("mod_bias", [P, 4, CH])
        mod = sb("mod", [P, 4, CH, B])
        eps = sb("eps", [P, BLK])
        minus_half = sb("minus_half", [P, BLK])

        x_in = sb("x_in", [P, BLK, D])
        ms1 = sb("ms1", [P, BLK])
        mse1 = sb("mse1", [P, BLK])
        inv1 = sb("inv1", [P, BLK])
        x_scaled1 = sb("x_scaled1", [P, BLK, D])
        xn1 = sb("xn1", [P, CH, TOK])
        xn1_hi = sb("xn1_hi", [P, CH, TOK], F32R)
        xn1_lo = sb("xn1_lo", [P, CH, TOK], F32R)
        q_masked = sb("q_masked", [P, CH, SEQS, 2, L])
        kT = sb("kT", [P, CH, TOK])
        values = sb("values", [P, BLK, PAIRS, VW])
        row_max = sb("row_max", [P, SEQS])
        shifted = sb("shifted", [P, TOK])
        probsT = sb("probsT", [P, 2, TOK])
        recip = sb("recip", [P, SEQS])
        att = sb("att", [P, SEQS, PAIRS, DH])
        attT_hi = sb("attT_hi", [P, 2, TOK], F32R)
        attT_lo = sb("attT_lo", [P, 2, TOK], F32R)
        x_res = sb("x_res", [P, BLK, D])
        x1 = sb("x1", [P, BLK, D])
        x_plus_x1 = sb("x_plus_x1", [P, BLK, D])
        ms2 = sb("ms2", [P, BLK])
        mse2 = sb("mse2", [P, BLK])
        inv2 = sb("inv2", [P, BLK])
        x_scaled2 = sb("x_scaled2", [P, BLK, D])
        xn2 = sb("xn2", [P, CH, TOK])
        xn2_hi = sb("xn2_hi", [P, CH, TOK], F32R)
        xn2_lo = sb("xn2_lo", [P, CH, TOK], F32R)
        tanh_g = sb("tanh_g", [P, TOK])
        silu2 = sb("silu2", [P, TOK])
        h = sb("h", [P, TOK])
        h_hi = sb("h_hi", [P, 2, TOK], F32R)
        h_lo = sb("h_lo", [P, 2, TOK], F32R)
        result = sb("result", [P, BLK, D])

        consts_in, mod_in, att_w_in, gate_w_in, hid_w_in, out_w_in = map(
            sem, ["consts_in", "mod_in", "att_w_in", "gate_w_in", "hid_w_in", "out_w_in"])
        w_hi_done, w_lo_done = sem("w_hi_done"), sem("w_lo_done")
        mod_mm, mod_done, powers_set, values_zeroed, values_set = map(
            sem, ["mod_mm", "mod_done", "powers_set", "values_zeroed", "values_set"])
        x_loaded, x_res_done, stored = sem("x_loaded"), sem("x_res_done"), sem("stored")
        ms1_done, mse1_done, inv1_done, scaled1 = map(sem, ["ms1_done", "mse1_done", "inv1_done", "scaled1"])
        xT1_done, gained1, xn1_done, xn1_hi_done, xn1_lo_done = map(
            sem, ["xT1_done", "gained1", "xn1_done", "xn1_hi_done", "xn1_lo_done"])
        q_mm, q_done, k_mm, k_done, v_mm, v_even, v_odd = map(
            sem, ["q_mm", "q_done", "k_mm", "k_done", "v_mm", "v_even", "v_odd"])
        score_mm, max_done, shift_done, shiftT_done, exp_done, pv_mm, recip_done, att_done = map(
            sem, ["score_mm", "max_done", "shift_done", "shiftT_done", "exp_done", "pv_mm", "recip_done", "att_done"])
        attT_mm, attT_hi_done, attT_lo_done, proj_mm, x1_done, sum_done = map(
            sem, ["attT_mm", "attT_hi_done", "attT_lo_done", "proj_mm", "x1_done", "sum_done"])
        ms2_done, mse2_done, inv2_done, scaled2 = map(sem, ["ms2_done", "mse2_done", "inv2_done", "scaled2"])
        xT2_done, gained2, xn2_done, xn2_hi_done, xn2_lo_done = map(
            sem, ["xT2_done", "gained2", "xn2_done", "xn2_hi_done", "xn2_lo_done"])
        gate_mm, hid_mm, tanh_done, silu_done, h_done, h_hi_done, h_lo_done, down_mm, result_done = map(
            sem, ["gate_mm", "hid_mm", "tanh_done", "silu_done", "h_done", "h_hi_done", "h_lo_done",
                  "down_mm", "result_done"])

        def wait(eng, semaphore, count):
            if not isinstance(count, int) or count > 0:
                eng.wait_ge(semaphore, count)

        def over_tiles(eng, iteration):
            iteration(0, attend=True, mlp=False, ahead=True)
            iteration(1, attend=True, mlp=True, ahead=True)
            with eng.Fori(2, TILES - 1) as t:
                iteration(t, attend=True, mlp=True, ahead=True)
            iteration(TILES - 1, attend=True, mlp=True, ahead=False)
            iteration(TILES, attend=False, mlp=True, ahead=False)

        block = ctx.enter_context(nc.Block())

        @block.sync
        def _(sp):
            sp.dma_start(x_in[:, :, :], x_t[0]).then_inc(x_loaded, 16)
            sp.dma_start(ident_mask[:, :], consts).then_inc(consts_in, 16)
            for m, w in enumerate((WqT, WkT, WvT, WoT)):
                sp.dma_start(raw[:, 0, m * CH * D:(m + 1) * CH * D].rearrange("p (c n) -> p c n", c=CH),
                             w.rearrange("(c p) n -> p c n", p=P)).then_inc(att_w_in, 16)
            sp.dma_start(cond_sb[:, :], condT).then_inc(mod_in, 16)
            for m, (w, b) in enumerate(((g1wT, g1b), (b1wT, b1b), (g2wT, g2b), (b2wT, b2b))):
                sp.dma_start(mod_w[:, m, :], w).then_inc(mod_in, 16)
                sp.dma_start(mod_bias[:, m, :], b).then_inc(mod_in, 16)
            sp.dma_start(raw[:, 1, :].rearrange("p (c n) -> p c n", c=CH),
                         gateT.rearrange("(c p) n -> p c n", p=P)).then_inc(gate_w_in, 16)
            sp.wait_ge(w_lo_done, 1)
            sp.dma_start(raw[:, 0, :].rearrange("p (c n) -> p c n", c=CH),
                         hidT.rearrange("(c p) n -> p c n", p=P)).then_inc(hid_w_in, 16)
            sp.wait_ge(w_lo_done, 2)
            sp.dma_start(raw[:, 1, :].rearrange("p (j n) -> p j n", j=CHUNKS),
                         outT.rearrange("(j p) n -> p j n", p=P)).then_inc(out_w_in, 16)

            def iteration(t, attend, mlp, ahead):
                if ahead:
                    sp.wait_ge(x_res_done, t + 1)
                    sp.wait_ge(scaled1, t + 1)
                    sp.dma_start(x_in[:, :, :], x_t[t + 1]).then_inc(x_loaded, 16)
                if mlp:
                    sp.wait_ge(result_done, 2 * t)
                    sp.dma_start(out_t[t - 1], result[:, :, :]).then_inc(stored, 16)

            over_tiles(sp, iteration)
            sp.wait_ge(stored, 16 * TILES)

        @block.gpsimd
        def _(pool):
            pool.memset(eps[:, :], EPS).then_inc(powers_set, 1)
            pool.memset(minus_half[:, :], -0.5).then_inc(powers_set, 1)
            pool.memset(values[:, :, :, :], 0.0).then_inc(values_zeroed, 1)
            pool.wait_ge(values_zeroed, 1)
            pool.memset(values[0:L, :, :, VW - 2:VW - 1], 1.0).then_inc(values_set, 1)
            pool.memset(values[L:P, :, :, VW - 1:VW], 1.0).then_inc(values_set, 1)
            pool.wait_ge(powers_set, 2)
            pool.wait_ge(values_set, 2)

            def inverse_rms(u, ms, ms_done, mse, mse_done, inv, inv_done, scaled):
                pool.wait_ge(ms_done, u + 1)
                nc.gpsimd.tensor_tensor(mse[:, :], ms[:, :], eps[:, :], ALU.add).then_inc(mse_done, 1)
                pool.wait_ge(mse_done, u + 1)
                wait(pool, scaled, u)
                nc.gpsimd.tensor_tensor(inv[:, :], mse[:, :], minus_half[:, :], ALU.pow).then_inc(inv_done, 1)

            def low_norm(u, c, xn, xn_hi, xn_lo, hi_done, lo_done, used, uses):
                pool.wait_ge(hi_done, CH * u + c + 1)
                wait(pool, used, uses)
                nc.gpsimd.tensor_tensor(xn_lo[:, c, :], xn[:, c, :], xn_hi[:, c, :].bitcast(F32),
                                        ALU.subtract).then_inc(lo_done, 1)

            def low_norm1(u, c):
                low_norm(u, c, xn1, xn1_hi, xn1_lo, xn1_hi_done, xn1_lo_done, v_mm, u)

            def low_norm2(u, c):
                low_norm(u, c, xn2, xn2_hi, xn2_lo, xn2_hi_done, xn2_lo_done, hid_mm, CHUNKS * u)

            def low_hidden(u, j):
                pool.wait_ge(h_hi_done, CHUNKS * u + j + 1)
                wait(pool, down_mm, CHUNKS * u + j - 1)
                nc.gpsimd.tensor_tensor(h_lo[:, j % 2, :], h[:, :], h_hi[:, j % 2, :].bitcast(F32),
                                        ALU.subtract).then_inc(h_lo_done, 1)

            inverse_rms(0, ms1, ms1_done, mse1, mse1_done, inv1, inv1_done, scaled1)
            for c in range(CH):
                low_norm1(0, c)

            def iteration(t, attend, mlp, ahead):
                for p in range(PAIRS):
                    if mlp and p == 0:
                        for c in range(CH):
                            low_norm2(t - 1, c)
                    if mlp and p >= 1:
                        low_hidden(t - 1, p - 1)
                    if ahead and p == 2:
                        inverse_rms(t + 1, ms1, ms1_done, mse1, mse1_done, inv1, inv1_done, scaled1)
                    if ahead and p >= 6:
                        low_norm1(t + 1, p - 6)
                if mlp:
                    low_hidden(t - 1, CHUNKS - 1)
                if attend:
                    inverse_rms(t, ms2, ms2_done, mse2, mse2_done, inv2, inv2_done, scaled2)
                    pool.wait_ge(x1_done, 2 * t + 2)
                    pool.wait_ge(x_res_done, t + 1)
                    wait(pool, result_done, 2 * t)
                    nc.gpsimd.tensor_tensor(x_plus_x1[:, :, :], x1[:, :, :], x_res[:, :, :],
                                            ALU.add).then_inc(sum_done, 1)

            over_tiles(pool, iteration)

        @block.scalar
        def _(act):
            def high_weights(n, landed, count, hi, piece):
                act.wait_ge(landed, count)
                nc.scalar.copy(hi, raw[:, piece, :]).then_inc(w_hi_done, 1)

            def mean_squares(u, src, ready, count, squares, transposed, ms, ms_done):
                act.wait_ge(ready, count)
                wait(act, transposed, CH * u)
                for k in range(BLK):
                    last = nc.scalar.activation(squares[:, k, :], src[:, k, :], ACT.Square, scale=float(D) ** -0.5,
                                                accum_out=ms[:, k:k + 1])
                last.then_inc(ms_done, 1)

            def high_norm1(u, c):
                act.wait_ge(xn1_done, CH * u + c + 1)
                wait(act, v_mm, u)
                nc.scalar.copy(xn1_hi[:, c, :], xn1[:, c, :]).then_inc(xn1_hi_done, 1)

            def high_norm2(u, c):
                act.wait_ge(xn2_done, CH * u + c + 1)
                wait(act, hid_mm, CHUNKS * u)
                nc.scalar.copy(xn2_hi[:, c, :], xn2[:, c, :]).then_inc(xn2_hi_done, 1)

            def masked_q(u):
                wait(act, score_mm, PAIRS * u)
                for c in range(CH):
                    act.wait_ge(q_mm, CH * u + c + 1)
                    for head in range(2):
                        last = nc.scalar.activation(q_masked[:, c, :, head, :],
                                                    ps[:, GATE + c, :].rearrange("p (b q) -> p b q", q=L), ACT.Copy,
                                                    scale=ident_mask[:, P + head:P + head + 1])
                    last.then_inc(q_done, 1)

            def even_values(u):
                act.wait_ge(v_mm, u + 1)
                wait(act, pv_mm, PAIRS * u)
                if isinstance(u, int) and u == 0:
                    act.wait_ge(values_set, 2)
                nc.scalar.copy(values[0:L, :, :, 0:ROWS],
                               ps[0:L, GATE:HIDDEN + 1, :].rearrange("p g (k n d) -> p (g k) n d", k=2, d=ROWS)
                               ).then_inc(v_even, 1)

            def tanh(u, j):
                act.wait_ge(gate_mm, CHUNKS * u + j + 1)
                wait(act, silu_done, CHUNKS * u + j)
                nc.scalar.activation(tanh_g[:, :], ps[:, GATE, :], ACT.Tanh, scale=0.5).then_inc(tanh_done, 1)

            def high_hidden(u, j):
                act.wait_ge(h_done, CHUNKS * u + j + 1)
                wait(act, down_mm, CHUNKS * u + j - 1)
                nc.scalar.copy(h_hi[:, j % 2, :], h[:, :]).then_inc(h_hi_done, 1)

            def exp(t, p):
                act.wait_ge(shiftT_done, PAIRS * t + p + 1)
                wait(act, pv_mm, PAIRS * t + p - 1)
                nc.scalar.activation(probsT[:, p % 2, :], ps[:, TRANS, :], ACT.Exp).then_inc(exp_done, 1)

            mean_squares(0, x_in, x_loaded, 16, x_scaled1, xT1_done, ms1, ms1_done)
            high_weights(0, att_w_in, 64, att_w_hi[:, :, :, :].rearrange("p m c n -> p (m c n)"), 0)
            act.wait_ge(consts_in, 16)
            for c in range(CH):
                high_norm1(0, c)
            masked_q(0)
            even_values(0)
            high_weights(1, gate_w_in, 16, gate_w_hi[:, :, :].rearrange("p c n -> p (c n)"), 1)
            high_weights(2, hid_w_in, 16, hid_w_hi[:, :, :].rearrange("p c n -> p (c n)"), 0)
            high_weights(3, out_w_in, 16, out_w_hi[:, :, :].rearrange("p j n -> p (j n)"), 1)

            def iteration(t, attend, mlp, ahead):
                for p in range(PAIRS):
                    if mlp and p >= 1:
                        tanh(t - 1, p - 1)
                    if attend:
                        exp(t, p)
                    if mlp and p == 0:
                        for c in range(CH):
                            high_norm2(t - 1, c)
                    if mlp and p >= 1:
                        high_hidden(t - 1, p - 1)
                    if attend and p == 1:
                        wait(act, sum_done, t)
                        wait(act, x1_done, 2 * t)
                        act.wait_ge(x_loaded, 16 * t + 16)
                        nc.scalar.copy(x_res[:, :, :], x_in[:, :, :]).then_inc(x_res_done, 1)
                    if ahead and p == 2:
                        mean_squares(t + 1, x_in, x_loaded, 16 * t + 32, x_scaled1, xT1_done, ms1, ms1_done)
                    if ahead and p >= 6:
                        high_norm1(t + 1, p - 6)
                if mlp:
                    tanh(t - 1, CHUNKS - 1)
                    high_hidden(t - 1, CHUNKS - 1)
                if ahead:
                    masked_q(t + 1)
                if attend:
                    for half in range(2):
                        act.wait_ge(attT_mm, 2 * t + half + 1)
                        wait(act, proj_mm, 2 * t)
                        nc.scalar.copy(
                            attT_hi[:, :, half * 256:half * 256 + 256].rearrange("p h (b q) -> p b h q", q=L),
                            ps[:, SCORE + half, :].rearrange("p (b h q) -> p b h q", h=2, q=L),
                        ).then_inc(attT_hi_done, 1)
                    mean_squares(t, x1, x1_done, 2 * t + 2, x_scaled2, xT2_done, ms2, ms2_done)
                if ahead:
                    even_values(t + 1)

            over_tiles(act, iteration)

        @block.vector
        def _(dve):
            def low_weights(n, lo, hi, piece):
                dve.wait_ge(w_hi_done, n + 1)
                nc.vector.tensor_tensor(lo, raw[:, piece, :], hi.bitcast(F32), ALU.subtract).then_inc(w_lo_done, 1)

            def scale_rows(u, src, inv, inv_done, dst, transposed, scaled):
                dve.wait_ge(inv_done, u + 1)
                wait(dve, transposed, CH * u)
                for k in range(BLK):
                    last = nc.vector.tensor_scalar(dst[:, k, :], src[:, k, :], inv[:, k:k + 1], None, ALU.mult)
                last.then_inc(scaled, 1)

            def of_sequences(m, c, u):
                return mod[:, m, c, bass.ds(u * SEQS, SEQS)].unsqueeze(2).to_broadcast([P, SEQS, L])

            def modulate(u, c, m, bank, transposed, xn, xn_lo_done, gained, done):
                dve.wait_ge(transposed, CH * u + c + 1)
                wait(dve, xn_lo_done, CH * u)
                dst = xn[:, c, :].rearrange("p (b q) -> p b q", q=L)
                nc.vector.tensor_tensor(dst, ps[:, bank, :].rearrange("p (b q) -> p b q", q=L),
                                        of_sequences(m, c, u), ALU.mult).then_inc(gained, 1)
                dve.wait_ge(gained, CH * u + c + 1)
                nc.vector.tensor_tensor(dst, dst, of_sequences(m + 1, c, u), ALU.add).then_inc(done, 1)

            def copy_k(u):
                wait(dve, score_mm, PAIRS * u)
                for c in range(CH):
                    dve.wait_ge(k_mm, CH * u + c + 1)
                    nc.vector.tensor_copy(kT[:, c, :], ps[:, OUT + c, :]).then_inc(k_done, 1)

            def odd_values(u):
                dve.wait_ge(v_mm, u + 1)
                wait(dve, pv_mm, PAIRS * u)
                if isinstance(u, int) and u == 0:
                    dve.wait_ge(values_set, 2)
                nc.vector.tensor_copy(values[L:P, :, :, ROWS:2 * ROWS],
                                      ps[L:P, GATE:HIDDEN + 1, :].rearrange("p g (k n d) -> p (g k) n d", k=2, d=ROWS)
                                      ).then_inc(v_odd, 1)

            def reciprocals(t, p):
                dve.wait_ge(pv_mm, PAIRS * t + p + 1)
                sums = ps[:, OUT, 0:BLK * VW].rearrange("p (k n) -> p k n", n=VW)[:, :, VW - 2:VW]
                nc.vector.reciprocal(recip[:, :].rearrange("p (k s) -> p k s", s=2), sums).then_inc(recip_done, 1)

            def normalise(t, p):
                dve.wait_ge(recip_done, PAIRS * t + p + 1)
                wait(dve, attT_mm, 2 * t)
                for head in range(2):
                    rows = slice(head * L, head * L + L)
                    own = ps[rows, OUT, 0:BLK * VW].rearrange("p (k n) -> p k n", n=VW)[:, :, 0:2 * ROWS].rearrange(
                        "p k (s h d) -> p k s h d", s=2, h=2)[:, :, :, head, :]
                    last = nc.vector.tensor_tensor(
                        att[rows, :, p, :].rearrange("p (k s) d -> p k s d", s=2), own,
                        recip[rows, :].rearrange("p (k s) -> p k s", s=2).unsqueeze(3).to_broadcast([L, BLK, 2, DH]),
                        ALU.mult)
                last.then_inc(att_done, 1)

            def row_maxima(t, p):
                dve.wait_ge(score_mm, PAIRS * t + p + 1)
                nc.vector.tensor_reduce(row_max[:, :], ps[:, SCORE, :].rearrange("p (b k) -> p b k", k=L),
                                        AX_X, ALU.max).then_inc(max_done, 1)

            def shift(t, p):
                dve.wait_ge(max_done, PAIRS * t + p + 1)
                wait(dve, shiftT_done, PAIRS * t + p)
                nc.vector.tensor_tensor(shifted[:, :].rearrange("p (b k) -> p b k", k=L),
                                        ps[:, SCORE, :].rearrange("p (b k) -> p b k", k=L),
                                        row_max[:, :].unsqueeze(2).to_broadcast([P, SEQS, L]),
                                        ALU.subtract).then_inc(shift_done, 1)

            def silu(u, j):
                dve.wait_ge(tanh_done, CHUNKS * u + j + 1)
                nc.vector.scalar_tensor_tensor(silu2[:, :], tanh_g[:, :], 1.0, ps[:, GATE, :],
                                               ALU.add, ALU.mult).then_inc(silu_done, 1)

            def hidden(u, j):
                dve.wait_ge(silu_done, CHUNKS * u + j + 1)
                dve.wait_ge(hid_mm, CHUNKS * u + j + 1)
                wait(dve, h_lo_done, CHUNKS * u + j)
                nc.vector.scalar_tensor_tensor(h[:, :], silu2[:, :], 0.5, ps[:, HIDDEN, :],
                                               ALU.mult, ALU.mult).then_inc(h_done, 1)

            scale_rows(0, x_in, inv1, inv1_done, x_scaled1, xT1_done, scaled1)
            low_weights(0, att_w_lo[:, :, :, :].rearrange("p m c n -> p (m c n)"),
                        att_w_hi[:, :, :, :].rearrange("p m c n -> p (m c n)"), 0)
            dve.wait_ge(mod_in, 9 * 16)
            for m in range(4):
                for c in range(CH):
                    dve.wait_ge(mod_mm, 2 * CH * (m // 2 + 1))
                    nc.vector.tensor_scalar(mod[:, m, c, :], ps[:, Y + m // 2, ((m % 2) * CH + c) * B:((m % 2) * CH + c + 1) * B],
                                            mod_bias[:, m, c:c + 1], None, ALU.add).then_inc(mod_done, 1)
            dve.wait_ge(mod_done, 4 * CH)
            for c in range(CH):
                modulate(0, c, 0, SCORE + c, xT1_done, xn1, xn1_lo_done, gained1, xn1_done)
            copy_k(0)
            odd_values(0)
            low_weights(1, gate_w_lo[:, :, :].rearrange("p c n -> p (c n)"),
                        gate_w_hi[:, :, :].rearrange("p c n -> p (c n)"), 1)
            low_weights(2, hid_w_lo[:, :, :].rearrange("p c n -> p (c n)"),
                        hid_w_hi[:, :, :].rearrange("p c n -> p (c n)"), 0)
            low_weights(3, out_w_lo[:, :, :].rearrange("p j n -> p (j n)"),
                        out_w_hi[:, :, :].rearrange("p j n -> p (j n)"), 1)

            def iteration(t, attend, mlp, ahead):
                for p in range(PAIRS):
                    if attend and p >= 2:
                        reciprocals(t, p - 2)
                    if attend:
                        row_maxima(t, p)
                    if attend and p >= 2:
                        normalise(t, p - 2)
                    if attend:
                        shift(t, p)
                    if mlp and p == 0:
                        for c in range(CH):
                            modulate(t - 1, c, 2, OUT + c, xT2_done, xn2, xn2_lo_done, gained2, xn2_done)
                    if mlp and p >= 1:
                        silu(t - 1, p - 1)
                        hidden(t - 1, p - 1)
                    if ahead and p == 3:
                        scale_rows(t + 1, x_in, inv1, inv1_done, x_scaled1, xT1_done, scaled1)
                    if ahead and p in (5, 6):
                        modulate(t + 1, p - 5, 0, EXTRA, xT1_done, xn1, xn1_lo_done, gained1, xn1_done)
                if attend:
                    reciprocals(t, PAIRS - 2)
                    normalise(t, PAIRS - 2)
                if mlp:
                    silu(t - 1, CHUNKS - 1)
                    hidden(t - 1, CHUNKS - 1)
                if attend:
                    reciprocals(t, PAIRS - 1)
                    normalise(t, PAIRS - 1)
                if mlp:
                    dve.wait_ge(down_mm, CHUNKS * t)
                    dve.wait_ge(sum_done, t)
                    wait(dve, stored, 16 * (t - 1))
                    for half in range(2):
                        nc.vector.tensor_tensor(result[:, 2 * half:2 * half + 2, :],
                                                ps[:, Y + half, :].rearrange("p (k n) -> p k n", k=2),
                                                x_plus_x1[:, 2 * half:2 * half + 2, :], ALU.add).then_inc(result_done, 1)
                if attend:
                    for half in range(2):
                        dve.wait_ge(attT_hi_done, 2 * t + half + 1)
                        wait(dve, proj_mm, 2 * t)
                        cols = slice(half * 256, half * 256 + 256)
                        for head in range(2):
                            last = nc.vector.tensor_tensor(
                                attT_lo[:, head, cols].rearrange("p (b q) -> p b q", q=L),
                                ps[:, SCORE + half, :].rearrange("p (b h q) -> p b h q", h=2, q=L)[:, :, head, :],
                                attT_hi[:, head, cols].bitcast(F32).rearrange("p (b q) -> p b q", q=L), ALU.subtract)
                        last.then_inc(attT_lo_done, 1)
                if ahead:
                    copy_k(t + 1)
                if attend:
                    wait(dve, sum_done, t)
                    wait(dve, ms2_done, t)
                    dve.wait_ge(x_res_done, t + 1)
                    for half in range(2):
                        dve.wait_ge(proj_mm, 2 * t + half + 1)
                        nc.vector.tensor_tensor(x1[:, 2 * half:2 * half + 2, :],
                                                ps[:, Y + half, :].rearrange("p (k n) -> p k n", k=2),
                                                x_res[:, 2 * half:2 * half + 2, :], ALU.add).then_inc(x1_done, 1)
                if ahead:
                    odd_values(t + 1)
                if attend:
                    dve.wait_ge(x1_done, 2 * t + 2)
                    scale_rows(t, x1, inv2, inv2_done, x_scaled2, xT2_done, scaled2)

            over_tiles(dve, iteration)

        @block.tensor
        def _(pe):
            def three_passes(dst, a_hi, a_lo, b_hi, b_lo, first, last, skip=False):
                nc.tensor.matmul(dst, a_hi, b_hi, start=first, stop=False, skip_group_check=skip)
                nc.tensor.matmul(dst, a_hi, b_lo, start=False, stop=False, skip_group_check=skip)
                return nc.tensor.matmul(dst, a_lo, b_hi, start=False, stop=last, skip_group_check=skip)

            def transpose_norm1(u, c, bank):
                pe.wait_ge(scaled1, u + 1)
                for k in range(BLK):
                    last = nc.tensor.transpose(ps[:, bank, k * P:(k + 1) * P],
                                               x_scaled1[:, k, c * P:(c + 1) * P], ident)
                last.then_inc(xT1_done, 1)

            def channel_major(m, c, dst):
                for i in range(CH):
                    w = slice(c * P, (c + 1) * P)
                    last = three_passes(dst, att_w_hi[:, m, i, w], att_w_lo[:, m, i, w],
                                        xn1_hi[:, i, :], xn1_lo[:, i, :], i == 0, i == CH - 1)
                return last

            def project_q(u):
                pe.wait_ge(xn1_lo_done, CH * u + CH)
                for c in range(CH):
                    channel_major(0, c, ps[:, GATE + c, :]).then_inc(q_mm, 1)

            def project_k(u):
                for c in range(CH):
                    channel_major(1, c, ps[:, OUT + c, :]).then_inc(k_mm, 1)

            def project_v(u):
                pe.wait_ge(q_done, CH * u + CH)
                for k in range(BLK):
                    tok = slice(k * P, (k + 1) * P)
                    for i in range(CH):
                        last = three_passes(ps[:, GATE + k // 2, (k % 2) * D:(k % 2) * D + D],
                                            xn1_hi[:, i, tok], xn1_lo[:, i, tok],
                                            att_w_hi[:, 2, i, :], att_w_lo[:, 2, i, :], i == 0, i == CH - 1)
                last.then_inc(v_mm, 1)

            def scores(t, p):
                wait(pe, shift_done, PAIRS * t + p)
                c, rows = p // 4, slice(ROWS * (p % 4), ROWS * (p % 4) + ROWS)
                for b in range(SEQS):
                    tok = slice(b * L, (b + 1) * L)
                    last = nc.tensor.matmul(ps[:, SCORE, tok], q_masked[rows, c, b, :, :].rearrange("p h q -> p (h q)"), kT[rows, c, tok],
                                            start=True, stop=True, tile_position=(ROWS * (p % 4), 0))
                last.then_inc(score_mm, 1)

            def transpose_shifted(t, p):
                pe.wait_ge(shift_done, PAIRS * t + p + 1)
                wait(pe, exp_done, PAIRS * t + p)
                for k in range(BLK):
                    last = nc.tensor.transpose(ps[:, TRANS, k * P:(k + 1) * P], shifted[:, k * P:(k + 1) * P], ident)
                last.then_inc(shiftT_done, 1)

            def probs_values(t, p):
                pe.wait_ge(exp_done, PAIRS * t + p + 1)
                wait(pe, att_done, PAIRS * t + p)
                for k in range(BLK):
                    last = nc.tensor.matmul(ps[:, OUT, k * VW:(k + 1) * VW], probsT[:, p % 2, k * P:(k + 1) * P],
                                            values[:, k, p, :], start=True, stop=True)
                last.then_inc(pv_mm, 1)

            def gate_hidden(u, j):
                wait(pe, h_done, CHUNKS * u + j)
                w = slice(j * P, (j + 1) * P)
                for bank, hi, lo, done in ((GATE, gate_w_hi, gate_w_lo, gate_mm), (HIDDEN, hid_w_hi, hid_w_lo, hid_mm)):
                    for i in range(CH):
                        last = three_passes(ps[:, bank, :], hi[:, i, w], lo[:, i, w],
                                            xn2_hi[:, i, :], xn2_lo[:, i, :], i == 0, i == CH - 1)
                    last.then_inc(done, 1)

            def down(u, j):
                pe.wait_ge(h_lo_done, CHUNKS * u + j + 1)
                for k in range(BLK):
                    tok = slice(k * P, (k + 1) * P)
                    last = three_passes(ps[:, Y + k // 2, (k % 2) * D:(k % 2) * D + D],
                                        h_hi[:, j % 2, tok], h_lo[:, j % 2, tok],
                                        out_w_hi[:, j, :], out_w_lo[:, j, :],
                                        j == 0 and k % 2 == 0, j == CHUNKS - 1, skip=True)
                last.then_inc(down_mm, 1)

            pe.wait_ge(mod_in, 9 * 16)
            for m in range(4):
                for c in range(CH):
                    nc.tensor.matmul(ps[:, Y + m // 2, ((m % 2) * CH + c) * B:((m % 2) * CH + c + 1) * B],
                                     mod_w[:, m, c * P:(c + 1) * P], cond_sb[:, :], start=True, stop=True
                                     ).then_inc(mod_mm, 1)
            pe.wait_ge(consts_in, 16)
            for c in range(CH):
                transpose_norm1(0, c, SCORE + c)
            pe.wait_ge(w_lo_done, 1)
            project_q(0)
            project_k(0)
            project_v(0)

            def iteration(t, attend, mlp, ahead):
                if attend:
                    pe.wait_ge(q_done, CH * t + CH)
                    pe.wait_ge(k_done, CH * t + CH)
                for p in range(PAIRS):
                    if attend:
                        scores(t, p)
                    if mlp and p == 0:
                        pe.wait_ge(scaled2, t)
                        for c in range(CH):
                            for k in range(BLK):
                                last = nc.tensor.transpose(ps[:, OUT + c, k * P:(k + 1) * P],
                                                           x_scaled2[:, k, c * P:(c + 1) * P], ident)
                            last.then_inc(xT2_done, 1)
                    if mlp and p >= 1:
                        if p == 1:
                            wait(pe, v_even, t + 1 if attend else t)
                            wait(pe, v_odd, t + 1 if attend else t)
                            pe.wait_ge(xn2_lo_done, CH * t)
                            if isinstance(t, int) and t == 1:
                                pe.wait_ge(w_lo_done, 4)
                        gate_hidden(t - 1, p - 1)
                    if attend:
                        transpose_shifted(t, p)
                    if mlp and p >= 2:
                        down(t - 1, p - 2)
                    if attend and p >= 1:
                        if p == 1:
                            pe.wait_ge(v_even, t + 1)
                            pe.wait_ge(v_odd, t + 1)
                            wait(pe, gained2, CH * t)
                        probs_values(t, p - 1)
                    if ahead and p in (4, 5):
                        if p == 5:
                            pe.wait_ge(gained1, CH * t + CH + 1)
                        transpose_norm1(t + 1, p - 4, EXTRA)
                if mlp:
                    gate_hidden(t - 1, CHUNKS - 1)
                    down(t - 1, CHUNKS - 2)
                if attend:
                    probs_values(t, PAIRS - 1)
                if ahead:
                    wait(pe, h_done, CHUNKS * t)
                    project_q(t + 1)
                if mlp:
                    down(t - 1, CHUNKS - 1)
                if attend:
                    pe.wait_ge(att_done, PAIRS * t + PAIRS)
                    for half in range(2):
                        for b in range(SEQS // 2):
                            last = nc.tensor.transpose(
                                ps[:, SCORE + half, b * P:(b + 1) * P],
                                att[:, half * 4 + b, :, :].rearrange("p n d -> p (n d)"), ident)
                        last.then_inc(attT_mm, 1)
                if ahead:
                    project_k(t + 1)
                if attend:
                    wait(pe, result_done, 2 * t)
                    for k in range(BLK):
                        tok = slice(k * P, (k + 1) * P)
                        pe.wait_ge(attT_lo_done, 2 * t + k // 2 + 1)
                        for head in range(2):
                            last = three_passes(ps[:, Y + k // 2, (k % 2) * D:(k % 2) * D + D],
                                                attT_hi[:, head, tok], attT_lo[:, head, tok],
                                                att_w_hi[:, 3, head, :], att_w_lo[:, 3, head, :], head == 0, head == 1)
                        if k % 2:
                            last.then_inc(proj_mm, 1)
                if ahead:
                    project_v(t + 1)

            over_tiles(pe, iteration)


_NAMES = ["x", "condT", "WqT", "WkT", "WvT", "WoT", "g1wT", "g1b", "b1wT", "b1b", "g2wT", "g2b", "b2wT", "b2b",
          "gateT", "hidT", "outT", "consts"]


def kernel(**inputs):
    import numpy as np
    import concourse.bacc as bacc
    from concourse.bass_utils import run_bass_kernel_spmd

    a = {k.removeprefix("L0_cond_"): np.asarray(v) for k, v in inputs.items()}
    columns = lambda v: v.reshape(CH, P).T
    wo_rows = a["Wo"].T.reshape(PAIRS, 2, DH, D).transpose(1, 0, 2, 3).reshape(D, D)
    head_of_row = (np.arange(P) // DH) % 2
    consts = np.concatenate([np.eye(P), np.stack([(head_of_row == n) * 0.25 for n in range(2)], 1)], 1).astype(np.float32)
    laid = {
        "x": a["x"], "condT": a["cond_256"].T, "WqT": a["Wq"].T, "WkT": a["Wk"].T, "WvT": a["Wv"].T, "WoT": wo_rows,
        "g1wT": a["g1w"].T, "g1b": columns(a["g1b"]), "b1wT": a["b1w"].T, "b1b": columns(a["b1b"]),
        "g2wT": a["g2w"].T, "g2b": columns(a["g2b"]), "b2wT": a["b2w"].T, "b2b": columns(a["b2b"]),
        "gateT": a["gate_w"].T, "hidT": a["hid_w"].T, "outT": a["out_w"].T, "consts": consts,
    }
    nc = bacc.Bacc("TRN2", target_bir_lowering=False, num_devices=1)
    arrays, args = {}, []
    for name in _NAMES:
        v = np.ascontiguousarray(laid[name])
        arrays[f"in_{name}"] = v
        args.append(nc.dram_tensor(f"in_{name}", v.shape, mybir.dt.from_np(v.dtype), kind="ExternalInput").ap())
    args.append(nc.dram_tensor("out_0", (B, L, D), F32, kind="ExternalOutput").ap())
    conditioned_block(nc, *args)
    r = run_bass_kernel_spmd(nc, [arrays], core_ids=[0])
    return r.results[0]["out_0"]
```

```python
from contextlib import ExitStack

import concourse.bass as bass
from concourse import mybir

ALU = mybir.AluOpType
ACT = mybir.ActivationFunctionType
AX_X = mybir.AxisListType.X
F32 = mybir.dt.float32
F32R = mybir.dt.float32r

P = 128
B, L, D = 128, 64, 256
DT = 64
HEADS, DH = 16, 16
HID = 4 * D
EPS = 1e-6
SEQS = 8
TOK = SEQS * L
TILES = B // SEQS
BLK = TOK // P
CH = D // P
PAIRS = HEADS // 2
ROWS = 2 * DH
CHUNKS = HID // P
LAG = 2
VW = 2 * ROWS + 2

STACK = 3
ROUNDS = PAIRS // CH
FILL = 16 * 2 * STACK

GATE, HIDDEN, Y, SCORE, TRANS, OUT, EXTRA = 0, 1, 2, 4, 5, 6, 7


def conditioned_block(nc, x, condT, WqT, WkT, WvT, WoT, g1wT, g1b, b1wT, b1b, g2wT, g2b, b2wT, b2b,
                      gateT, hidT, outT, consts, out):
    x_t = x.rearrange("(t k s) l c -> t (s l) k c", k=BLK, s=P // L)
    out_t = out.rearrange("(t k s) l c -> t (s l) k c", k=BLK, s=P // L)

    with ExitStack() as ctx:
        def sb(name, shape, dt=F32):
            return ctx.enter_context(nc.sbuf_tensor(name, shape, dt))

        def sem(name):
            return ctx.enter_context(nc.semaphore(name))

        ps = ctx.enter_context(nc.psum_tensor("ps", [P, 8, 512], F32))

        ident_mask = sb("ident_mask", [P, P + 2])
        ident = ident_mask[:, 0:P]
        shared = sb("shared", [P, 4, BLK * D])
        raw = shared[:, :, :].rearrange("p (a b) n -> p a (b n)", a=2)
        att_w_hi = sb("att_w_hi", [P, 4, CH, D], F32R)
        att_w_lo = sb("att_w_lo", [P, 4, CH, D], F32R)
        gate_w_hi = sb("gate_w_hi", [P, CH, HID], F32R)
        gate_w_lo = sb("gate_w_lo", [P, CH, HID], F32R)
        hid_w_hi = sb("hid_w_hi", [P, CH, HID], F32R)
        hid_w_lo = sb("hid_w_lo", [P, CH, HID], F32R)
        out_w_hi = sb("out_w_hi", [P, CHUNKS, D], F32R)
        out_w_lo = sb("out_w_lo", [P, CHUNKS, D], F32R)
        cond_sb = sb("cond_sb", [DT, B])
        result = sb("result", [P, BLK, D])
        mod_w = result[0:DT, :, :]
        mod_bias = sb("mod_bias", [P, 4, CH])
        mod = sb("mod", [P, 4, CH, B])
        eps = sb("eps", [P, BLK])
        minus_half = sb("minus_half", [P, BLK])

        x_in = sb("x_in", [P, BLK, D])
        ms1 = sb("ms1", [P, BLK])
        mse1 = sb("mse1", [P, BLK])
        inv1 = sb("inv1", [P, BLK])
        x_scaled1 = sb("x_scaled1", [P, BLK, D])
        xn1 = sb("xn1", [P, CH, TOK])
        xn1_hi = sb("xn1_hi", [P, CH, TOK], F32R)
        xn1_lo = sb("xn1_lo", [P, CH, TOK], F32R)
        q_hi = sb("q_hi", [P, CH, SEQS, 2, L], F32R)
        q_lo = sb("q_lo", [P, CH, SEQS, 2, L], F32R)
        k_hi = sb("k_hi", [P, CH, TOK], F32R)
        k_lo = sb("k_lo", [P, CH, TOK], F32R)
        q_stack = sb("q_stack", [STACK * ROWS, 2, CH, SEQS, 2 * L], F32R)
        k_stack = sb("k_stack", [STACK * ROWS, 2, CH, TOK], F32R)
        values = sb("values", [P, BLK, PAIRS, VW])
        row_max = sb("row_max", [P, SEQS])
        shifted = sb("shifted", [P, TOK])
        probsT = sb("probsT", [P, 2, TOK])
        recip = sb("recip", [P, SEQS])
        att = sb("att", [P, SEQS, PAIRS, DH])
        attT_hi = sb("attT_hi", [P, 2, TOK], F32R)
        attT_lo = sb("attT_lo", [P, 2, TOK], F32R)
        x_res = sb("x_res", [P, BLK, D])
        x_plus_x1 = sb("x_plus_x1", [P, BLK, D])
        x1 = shared[:, 2, :].rearrange("p (k n) -> p k n", k=BLK)
        ms2 = sb("ms2", [P, BLK])
        mse2 = sb("mse2", [P, BLK])
        inv2 = sb("inv2", [P, BLK])
        x_scaled2 = shared[:, 0, :].rearrange("p (k n) -> p k n", k=BLK)
        xn2 = shared[:, 1, :].rearrange("p (c n) -> p c n", c=CH)
        xn2_hi = sb("xn2_hi", [P, CH, TOK], F32R)
        xn2_lo = sb("xn2_lo", [P, CH, TOK], F32R)
        act_g = shared[:, 3, 0:TOK]
        h = shared[:, 3, TOK:2 * TOK]
        h_hi = sb("h_hi", [P, 2, TOK], F32R)
        h_lo = sb("h_lo", [P, 2, TOK], F32R)

        consts_in, mod_in, att_w_in, gate_w_in, hid_w_in, out_w_in = map(
            sem, ["consts_in", "mod_in", "att_w_in", "gate_w_in", "hid_w_in", "out_w_in"])
        w_hi_done, att_w_split, mlp_w_split = sem("w_hi_done"), sem("att_w_split"), sem("mlp_w_split")
        mod_mm, mod_done, powers_set, values_zeroed, values_set = map(
            sem, ["mod_mm", "mod_done", "powers_set", "values_zeroed", "values_set"])
        x_loaded, x_res_done, stored = sem("x_loaded"), sem("x_res_done"), sem("stored")
        ms1_done, mse1_done, inv1_done, scaled1 = map(sem, ["ms1_done", "mse1_done", "inv1_done", "scaled1"])
        xT1_done, gained1, xn1_done, xn1_hi_done, xn1_lo_done = map(
            sem, ["xT1_done", "gained1", "xn1_done", "xn1_hi_done", "xn1_lo_done"])
        q_mm, q_hi_done, q_lo_done, k_mm, k_hi_done, k_lo_done, v_mm, v_even, v_odd = map(
            sem, ["q_mm", "q_hi_done", "q_lo_done", "k_mm", "k_hi_done", "k_lo_done", "v_mm", "v_even", "v_odd"])
        stacked = [sem("stacked_even"), sem("stacked_odd")]
        score_mm, max_done, shift_done, shiftT_done, exp_done, pv_mm, recip_done, att_done = map(
            sem, ["score_mm", "max_done", "shift_done", "shiftT_done", "exp_done", "pv_mm", "recip_done", "att_done"])
        attT_mm, attT_hi_done, attT_lo_done, proj_mm, x1_done, sum_done = map(
            sem, ["attT_mm", "attT_hi_done", "attT_lo_done", "proj_mm", "x1_done", "sum_done"])
        ms2_done, mse2_done, inv2_done, scaled2 = map(sem, ["ms2_done", "mse2_done", "inv2_done", "scaled2"])
        xT2_done, gained2, xn2_done, xn2_hi_done, xn2_lo_done = map(
            sem, ["xT2_done", "gained2", "xn2_done", "xn2_hi_done", "xn2_lo_done"])
        gate_mm, hid_mm, tanh_done, silu_done, h_done, h_hi_done, h_lo_done, down_mm, result_done = map(
            sem, ["gate_mm", "hid_mm", "tanh_done", "silu_done", "h_done", "h_hi_done", "h_lo_done",
                  "down_mm", "result_done"])

        def wait(eng, semaphore, count):
            if not isinstance(count, int) or count > 0:
                eng.wait_ge(semaphore, count)

        def over_tiles(eng, iteration):
            iteration(0, attend=True, mlp=False, finish=False, ahead=True)
            iteration(1, attend=True, mlp=True, finish=False, ahead=True)
            with eng.Fori(2, TILES - 1) as t:
                iteration(t, attend=True, mlp=True, finish=True, ahead=True)
            iteration(TILES - 1, attend=True, mlp=True, finish=True, ahead=False)
            iteration(TILES, attend=False, mlp=True, finish=True, ahead=False)
            iteration(TILES + 1, attend=False, mlp=False, finish=True, ahead=False)

        def pair_of(p):
            return (p % CH) * (PAIRS // CH) + p // CH

        block = ctx.enter_context(nc.Block())

        @block.sync
        def _(sp):
            sp.dma_start(x_in[:, :, :], x_t[0]).then_inc(x_loaded, 16)
            for m, w in enumerate((WqT, WkT, WvT, WoT)):
                sp.dma_start(raw[:, 0, m * CH * D:(m + 1) * CH * D].rearrange("p (c n) -> p c n", c=CH),
                             w.rearrange("(c p) n -> p c n", p=P)).then_inc(att_w_in, 16)
            sp.dma_start(raw[:, 1, :].rearrange("p (c n) -> p c n", c=CH),
                         gateT.rearrange("(c p) n -> p c n", p=P)).then_inc(gate_w_in, 16)
            sp.wait_ge(att_w_split, 1)
            sp.dma_start(raw[:, 0, :].rearrange("p (c n) -> p c n", c=CH),
                         hidT.rearrange("(c p) n -> p c n", p=P)).then_inc(hid_w_in, 16)
            sp.wait_ge(mlp_w_split, 1)
            sp.dma_start(raw[:, 1, :].rearrange("p (j n) -> p j n", j=CHUNKS),
                         outT.rearrange("(j p) n -> p j n", p=P)).then_inc(out_w_in, 16)

            def stack(u, r):
                if r < 2:
                    sp.wait_ge(k_lo_done, CH * u + CH)
                    sp.wait_ge(q_lo_done, CH * u + CH)
                wait(sp, score_mm, PAIRS * u + CH * (r - 1))
                rows = slice(ROWS * r, ROWS * r + ROWS)
                for s, (q, k) in enumerate(((q_hi, k_hi), (q_hi, k_lo), (q_lo, k_hi))):
                    to = slice(ROWS * s, ROWS * s + ROWS)
                    sp.dma_start(q_stack[to, r % 2, :, :, :].rearrange("p c b n -> p c (b n)").bitcast(F32),
                                 q[rows, :, :, :, :].rearrange("p c b h n -> p c (b h n)").bitcast(F32)
                                 ).then_inc(stacked[r % 2], 16)
                    sp.dma_start(k_stack[to, r % 2, :, :].bitcast(F32), k[rows, :, :].bitcast(F32)
                                 ).then_inc(stacked[r % 2], 16)

            stack(0, 0)
            stack(0, 1)

            def iteration(t, attend, mlp, finish, ahead):
                if attend:
                    stack(t, 2)
                if finish:
                    sp.wait_ge(result_done, 2 * (t - 1))
                    sp.dma_start(out_t[t - 2], result[:, :, :]).then_inc(stored, 16)
                if ahead:
                    sp.wait_ge(x_res_done, t + 1)
                    sp.wait_ge(scaled1, t + 1)
                    sp.dma_start(x_in[:, :, :], x_t[t + 1]).then_inc(x_loaded, 16)
                if attend:
                    stack(t, 3)
                if ahead:
                    stack(t + 1, 0)
                    stack(t + 1, 1)

            over_tiles(sp, iteration)
            sp.wait_ge(stored, 16 * TILES)

        @block.gpsimd
        def _(pool):
            pool.memset(eps[:, :], EPS).then_inc(powers_set, 1)
            pool.memset(minus_half[:, :], -0.5).then_inc(powers_set, 1)
            pool.memset(values[:, :, :, :], 0.0).then_inc(values_zeroed, 1)
            pool.wait_ge(values_zeroed, 1)
            pool.memset(values[0:L, :, :, VW - 2:VW - 1], 1.0).then_inc(values_set, 1)
            pool.memset(values[L:P, :, :, VW - 1:VW], 1.0).then_inc(values_set, 1)
            pool.wait_ge(powers_set, 2)
            pool.wait_ge(values_set, 2)

            def inverse_rms(u, ms, ms_done, mse, mse_done, inv, inv_done, scaled):
                pool.wait_ge(ms_done, u + 1)
                nc.gpsimd.tensor_tensor(mse[:, :], ms[:, :], eps[:, :], ALU.add).then_inc(mse_done, 1)
                pool.wait_ge(mse_done, u + 1)
                wait(pool, scaled, u)
                nc.gpsimd.tensor_tensor(inv[:, :], mse[:, :], minus_half[:, :], ALU.pow).then_inc(inv_done, 1)

            def low_norm(u, c, xn, xn_hi, xn_lo, hi_done, lo_done, used, uses):
                pool.wait_ge(hi_done, CH * u + c + 1)
                wait(pool, used, uses)
                nc.gpsimd.tensor_tensor(xn_lo[:, c, :], xn[:, c, :], xn_hi[:, c, :].bitcast(F32),
                                        ALU.subtract).then_inc(lo_done, 1)

            def low_norm1(u, c):
                low_norm(u, c, xn1, xn1_hi, xn1_lo, xn1_hi_done, xn1_lo_done, v_mm, 2 * u)

            def low_norm2(u, c):
                low_norm(u, c, xn2, xn2_hi, xn2_lo, xn2_hi_done, xn2_lo_done, hid_mm, CHUNKS * u)

            def low_hidden(u, j):
                pool.wait_ge(h_hi_done, CHUNKS * u + j + 1)
                wait(pool, down_mm, CHUNKS * u + j - 1)
                nc.gpsimd.tensor_tensor(h_lo[:, j % 2, :], h[:, :], h_hi[:, j % 2, :].bitcast(F32),
                                        ALU.subtract).then_inc(h_lo_done, 1)

            inverse_rms(0, ms1, ms1_done, mse1, mse1_done, inv1, inv1_done, scaled1)
            for c in range(CH):
                low_norm1(0, c)

            def low_weights(n, lo, hi, piece):
                pool.wait_ge(w_hi_done, n + 1)
                nc.gpsimd.tensor_tensor(lo, raw[:, piece, :], hi.bitcast(F32), ALU.subtract).then_inc(mlp_w_split, 1)

            low_weights(1, gate_w_lo[:, :, :].rearrange("p c n -> p (c n)"),
                        gate_w_hi[:, :, :].rearrange("p c n -> p (c n)"), 1)
            low_weights(2, hid_w_lo[:, :, :].rearrange("p c n -> p (c n)"),
                        hid_w_hi[:, :, :].rearrange("p c n -> p (c n)"), 0)
            low_weights(3, out_w_lo[:, :, :].rearrange("p j n -> p (j n)"),
                        out_w_hi[:, :, :].rearrange("p j n -> p (j n)"), 1)

            def iteration(t, attend, mlp, finish, ahead):
                for p in range(PAIRS):
                    if mlp and p == 1:
                        low_norm2(t - 1, 0)
                    if finish and p == 1:
                        low_hidden(t - 2, CHUNKS - 1)
                    if mlp and p == 1:
                        low_norm2(t - 1, 1)
                    if ahead and p == 7:
                        low_norm1(t + 1, 1)
                    if mlp and p >= LAG:
                        low_hidden(t - 1, p - LAG)
                    if ahead and p == 6:
                        low_norm1(t + 1, 0)
                    if ahead and p == 4:
                        inverse_rms(t + 1, ms1, ms1_done, mse1, mse1_done, inv1, inv1_done, scaled1)
                if attend:
                    inverse_rms(t, ms2, ms2_done, mse2, mse2_done, inv2, inv2_done, scaled2)
                if mlp:
                    low_hidden(t - 1, CHUNKS - 2)

            over_tiles(pool, iteration)

        @block.scalar
        def _(act):
            act.dma_start(cond_sb[:, :], condT).then_inc(mod_in, 16)
            for m, (w, b) in enumerate(((g1wT, g1b), (b1wT, b1b), (g2wT, g2b), (b2wT, b2b))):
                act.dma_start(mod_w[:, m, :], w).then_inc(mod_in, 16)
                act.dma_start(mod_bias[:, m, :], b).then_inc(mod_in, 16)
            act.dma_start(ident_mask[:, :], consts).then_inc(consts_in, 16)

            def high_weights(n, landed, count, hi, piece):
                act.wait_ge(landed, count)
                nc.scalar.copy(hi, raw[:, piece, :]).then_inc(w_hi_done, 1)

            def mean_squares(u, src, ready, counts, squares, transposed, ms, ms_done):
                wait(act, transposed, CH * u)
                for k in range(BLK):
                    if k % 2 == 0:
                        act.wait_ge(ready, counts[k // 2])
                    last = nc.scalar.activation(squares[:, k, :], src[:, k, :], ACT.Square, scale=float(D) ** -0.5,
                                                accum_out=ms[:, k:k + 1])
                last.then_inc(ms_done, 1)

            def high_norm1(u, c):
                act.wait_ge(xn1_done, CH * u + c + 1)
                wait(act, v_mm, 2 * u)
                nc.scalar.copy(xn1_hi[:, c, :], xn1[:, c, :]).then_inc(xn1_hi_done, 1)

            def high_norm2(u, c):
                act.wait_ge(xn2_done, CH * u + c + 1)
                wait(act, hid_mm, CHUNKS * u)
                nc.scalar.copy(xn2_hi[:, c, :], xn2[:, c, :]).then_inc(xn2_hi_done, 1)

            def high_k(u):
                for c in range(CH):
                    act.wait_ge(k_mm, CH * u + c + 1)
                    if c == 0:
                        wait(act, stacked[0], 2 * FILL * u)
                        wait(act, stacked[1], 2 * FILL * u)
                    nc.scalar.copy(k_hi[:, c, :], ps[:, SCORE + c, :]).then_inc(k_hi_done, 1)

            def high_q(u, c):
                act.wait_ge(q_mm, CH * u + c + 1)
                for head in range(2):
                    last = nc.scalar.activation(q_hi[:, c, :, head, :],
                                                ps[:, GATE + c, :].rearrange("p (b q) -> p b q", q=L), ACT.Copy,
                                                scale=ident_mask[:, P + head:P + head + 1])
                last.then_inc(q_hi_done, 1)

            def even_values(u, half):
                act.wait_ge(v_mm, 2 * u + half + 1)
                wait(act, pv_mm, PAIRS * u)
                if isinstance(u, int) and u == 0:
                    act.wait_ge(values_set, 2)
                nc.scalar.copy(values[0:L, 2 * half:2 * half + 2, :, 0:ROWS],
                               ps[0:L, SCORE + half, :].rearrange("p (k n d) -> p k n d", k=2, d=ROWS)
                               ).then_inc(v_even, 1)

            def tanh(u, j):
                act.wait_ge(gate_mm, CHUNKS * u + j + 1)
                wait(act, h_done, CHUNKS * u + j)
                nc.scalar.activation(act_g[:, :], ps[:, GATE, :], ACT.Tanh, scale=0.5).then_inc(tanh_done, 1)

            def high_hidden(u, j):
                act.wait_ge(h_done, CHUNKS * u + j + 1)
                wait(act, down_mm, CHUNKS * u + j - 1)
                nc.scalar.copy(h_hi[:, j % 2, :], h[:, :]).then_inc(h_hi_done, 1)

            def exp(t, p):
                act.wait_ge(shiftT_done, PAIRS * t + p + 1)
                wait(act, pv_mm, PAIRS * t + p - 1)
                nc.scalar.activation(probsT[:, p % 2, :], ps[:, TRANS, :], ACT.Exp).then_inc(exp_done, 1)

            mean_squares(0, x_in, x_loaded, (16, 16), x_scaled1, xT1_done, ms1, ms1_done)
            high_weights(0, att_w_in, 64, att_w_hi[:, :, :, :].rearrange("p m c n -> p (m c n)"), 0)
            act.wait_ge(consts_in, 16)
            for c in range(CH):
                high_norm1(0, c)
            high_weights(1, gate_w_in, 16, gate_w_hi[:, :, :].rearrange("p c n -> p (c n)"), 1)
            high_k(0)
            for c in range(CH):
                high_q(0, c)
            for half in range(2):
                even_values(0, half)

            def iteration(t, attend, mlp, finish, ahead):
                for p in range(PAIRS):
                    if ahead and p == 7:
                        high_norm1(t + 1, 1)
                    if mlp and p >= LAG:
                        tanh(t - 1, p - LAG)
                    if finish and p == 0:
                        tanh(t - 2, CHUNKS - 1)
                    if attend:
                        exp(t, p)
                    if not mlp and attend and p == 1:
                        high_weights(2, hid_w_in, 16, hid_w_hi[:, :, :].rearrange("p c n -> p (c n)"), 0)
                    if not mlp and attend and p == 3:
                        high_weights(3, out_w_in, 16, out_w_hi[:, :, :].rearrange("p j n -> p (j n)"), 1)
                    if mlp and p == 0:
                        high_norm2(t - 1, 0)
                    if finish and p == 0:
                        high_hidden(t - 2, CHUNKS - 1)
                    if mlp and p == 0:
                        high_norm2(t - 1, 1)
                    if ahead and p == 6:
                        high_norm1(t + 1, 0)
                    if mlp and p >= LAG:
                        high_hidden(t - 1, p - LAG)
                    if attend and p == 3:
                        wait(act, sum_done, t)
                        act.wait_ge(x_loaded, 16 * t + 16)
                        nc.scalar.copy(x_res[:, :, :], x_in[:, :, :]).then_inc(x_res_done, 1)
                    if ahead and p == 4:
                        mean_squares(t + 1, x_in, x_loaded, (16 * t + 32, 16 * t + 32), x_scaled1, xT1_done,
                                     ms1, ms1_done)
                if ahead:
                    high_k(t + 1)
                    high_q(t + 1, 0)
                if attend:
                    for half in range(2):
                        act.wait_ge(attT_mm, 2 * t + half + 1)
                        wait(act, proj_mm, 2 * t)
                        nc.scalar.copy(
                            attT_hi[:, :, half * 256:half * 256 + 256].rearrange("p h (b q) -> p b h q", q=L),
                            ps[:, OUT + half, :].rearrange("p (b h q) -> p b h q", h=2, q=L),
                        ).then_inc(attT_hi_done, 1)
                if ahead:
                    high_q(t + 1, 1)
                    for half in range(2):
                        even_values(t + 1, half)
                if attend:
                    mean_squares(t, x1, x1_done, (2 * t + 1, 2 * t + 2), x_scaled2, xT2_done, ms2, ms2_done)
                if mlp:
                    tanh(t - 1, CHUNKS - 2)
                    high_hidden(t - 1, CHUNKS - 2)

            over_tiles(act, iteration)

        @block.vector
        def _(dve):
            def scale_rows(u, src, inv, inv_done, dst, transposed, scaled):
                dve.wait_ge(inv_done, u + 1)
                wait(dve, transposed, CH * u)
                for k in range(BLK):
                    last = nc.vector.tensor_scalar(dst[:, k, :], src[:, k, :], inv[:, k:k + 1], None, ALU.mult)
                last.then_inc(scaled, 1)

            def of_sequences(m, c, u):
                return mod[:, m, c, bass.ds(u * SEQS, SEQS)].unsqueeze(2).to_broadcast([P, SEQS, L])

            def gain(u, c, m, bank, transposed, xn, xn_lo_done, gained):
                dve.wait_ge(transposed, CH * u + c + 1)
                wait(dve, xn_lo_done, CH * u)
                nc.vector.tensor_tensor(xn[:, c, :].rearrange("p (b q) -> p b q", q=L),
                                        ps[:, bank, :].rearrange("p (b q) -> p b q", q=L),
                                        of_sequences(m, c, u), ALU.mult).then_inc(gained, 1)

            def add_shift(u, c, m, xn, gained, done):
                dve.wait_ge(gained, CH * u + c + 1)
                dst = xn[:, c, :].rearrange("p (b q) -> p b q", q=L)
                nc.vector.tensor_tensor(dst, dst, of_sequences(m, c, u), ALU.add).then_inc(done, 1)

            def low_k(u):
                for c in range(CH):
                    dve.wait_ge(k_hi_done, CH * u + c + 1)
                    nc.vector.tensor_tensor(k_lo[:, c, :], ps[:, SCORE + c, :], k_hi[:, c, :].bitcast(F32),
                                            ALU.subtract).then_inc(k_lo_done, 1)

            def low_q(u, c):
                dve.wait_ge(q_hi_done, CH * u + c + 1)
                for head in range(2):
                    last = nc.vector.scalar_tensor_tensor(
                        q_lo[:, c, :, head, :], ps[:, GATE + c, :].rearrange("p (b q) -> p b q", q=L),
                        ident_mask[:, P + head:P + head + 1], q_hi[:, c, :, head, :].bitcast(F32),
                        ALU.mult, ALU.subtract)
                last.then_inc(q_lo_done, 1)

            def odd_values(u, half):
                dve.wait_ge(v_mm, 2 * u + half + 1)
                wait(dve, pv_mm, PAIRS * u)
                if isinstance(u, int) and u == 0:
                    dve.wait_ge(values_set, 2)
                nc.vector.tensor_copy(values[L:P, 2 * half:2 * half + 2, :, ROWS:2 * ROWS],
                                      ps[L:P, SCORE + half, :].rearrange("p (k n d) -> p k n d", k=2, d=ROWS)
                                      ).then_inc(v_odd, 1)

            def reciprocals(t, p):
                dve.wait_ge(pv_mm, PAIRS * t + p + 1)
                sums = ps[:, OUT, 0:BLK * VW].rearrange("p (k n) -> p k n", n=VW)[:, :, VW - 2:VW]
                nc.vector.reciprocal(recip[:, :].rearrange("p (k s) -> p k s", s=2), sums).then_inc(recip_done, 1)

            def normalise(t, p):
                dve.wait_ge(recip_done, PAIRS * t + p + 1)
                wait(dve, attT_mm, 2 * t)
                for head in range(2):
                    rows = slice(head * L, head * L + L)
                    own = ps[rows, OUT, 0:BLK * VW].rearrange("p (k n) -> p k n", n=VW)[:, :, 0:2 * ROWS].rearrange(
                        "p k (s h d) -> p k s h d", s=2, h=2)[:, :, :, head, :]
                    last = nc.vector.tensor_tensor(
                        att[rows, :, pair_of(p), :].rearrange("p (k s) d -> p k s d", s=2), own,
                        recip[rows, :].rearrange("p (k s) -> p k s", s=2).unsqueeze(3).to_broadcast([L, BLK, 2, DH]),
                        ALU.mult)
                last.then_inc(att_done, 1)

            def row_maxima(t, p):
                dve.wait_ge(score_mm, PAIRS * t + p + 1)
                nc.vector.tensor_reduce(row_max[:, :], ps[:, SCORE, :].rearrange("p (b k) -> p b k", k=L),
                                        AX_X, ALU.max).then_inc(max_done, 1)

            def shift(t, p):
                dve.wait_ge(max_done, PAIRS * t + p + 1)
                wait(dve, shiftT_done, PAIRS * t + p)
                nc.vector.tensor_tensor(shifted[:, :].rearrange("p (b k) -> p b k", k=L),
                                        ps[:, SCORE, :].rearrange("p (b k) -> p b k", k=L),
                                        row_max[:, :].unsqueeze(2).to_broadcast([P, SEQS, L]),
                                        ALU.subtract).then_inc(shift_done, 1)

            def silu(u, j):
                dve.wait_ge(tanh_done, CHUNKS * u + j + 1)
                nc.vector.scalar_tensor_tensor(act_g[:, :], act_g[:, :], 1.0, ps[:, GATE, :],
                                               ALU.add, ALU.mult).then_inc(silu_done, 1)

            def hidden(u, j):
                dve.wait_ge(silu_done, CHUNKS * u + j + 1)
                dve.wait_ge(hid_mm, CHUNKS * u + j + 1)
                wait(dve, h_lo_done, CHUNKS * u + j)
                nc.vector.scalar_tensor_tensor(h[:, :], act_g[:, :], 0.5, ps[:, HIDDEN, :],
                                               ALU.mult, ALU.mult).then_inc(h_done, 1)

            scale_rows(0, x_in, inv1, inv1_done, x_scaled1, xT1_done, scaled1)
            dve.wait_ge(w_hi_done, 1)
            nc.vector.tensor_tensor(att_w_lo[:, :, :, :].rearrange("p m c n -> p (m c n)"), raw[:, 0, :],
                                    att_w_hi[:, :, :, :].rearrange("p m c n -> p (m c n)").bitcast(F32),
                                    ALU.subtract).then_inc(att_w_split, 1)
            dve.wait_ge(mod_in, 9 * 16)
            for m in range(4):
                for c in range(CH):
                    dve.wait_ge(mod_mm, 2 * CH * (m // 2 + 1))
                    at = ((m % 2) * CH + c) * B
                    nc.vector.tensor_scalar(mod[:, m, c, :], ps[:, Y + m // 2, at:at + B],
                                            mod_bias[:, m, c:c + 1], None, ALU.add).then_inc(mod_done, 1)
            dve.wait_ge(mod_done, 4 * CH)
            for c in range(CH):
                gain(0, c, 0, SCORE + c, xT1_done, xn1, xn1_lo_done, gained1)
                add_shift(0, c, 1, xn1, gained1, xn1_done)
            dve.wait_ge(consts_in, 16)
            low_k(0)
            for c in range(CH):
                low_q(0, c)
            for half in range(2):
                odd_values(0, half)

            def iteration(t, attend, mlp, finish, ahead):
                for p in range(PAIRS):
                    if ahead and p == 7:
                        gain(t + 1, 1, 0, EXTRA, xT1_done, xn1, xn1_lo_done, gained1)
                        add_shift(t + 1, 1, 1, xn1, gained1, xn1_done)
                    if attend and p >= 3:
                        reciprocals(t, p - 2)
                    if attend:
                        row_maxima(t, p)
                    if attend and p >= 3:
                        normalise(t, p - 2)
                    if attend:
                        shift(t, p)
                    if mlp and p == 0:
                        gain(t - 1, 0, 2, EXTRA, xT2_done, xn2, xn2_lo_done, gained2)
                        add_shift(t - 1, 0, 3, xn2, gained2, xn2_done)
                    if finish and p == 0:
                        silu(t - 2, CHUNKS - 1)
                        hidden(t - 2, CHUNKS - 1)
                    if mlp and p == 1:
                        gain(t - 1, 1, 2, EXTRA, xT2_done, xn2, xn2_lo_done, gained2)
                        add_shift(t - 1, 1, 3, xn2, gained2, xn2_done)
                    if attend and p == 1:
                        reciprocals(t, 0)
                        normalise(t, 0)
                    if finish and p == 2:
                        dve.wait_ge(down_mm, CHUNKS * (t - 1))
                        dve.wait_ge(sum_done, t - 1)
                        wait(dve, stored, 16 * (t - 2))
                        for half in range(2):
                            nc.vector.tensor_tensor(result[:, 2 * half:2 * half + 2, :],
                                                    ps[:, Y + half, :].rearrange("p (k n) -> p k n", k=2),
                                                    x_plus_x1[:, 2 * half:2 * half + 2, :],
                                                    ALU.add).then_inc(result_done, 1)
                    if mlp and p == 2:
                        dve.wait_ge(x1_done, 2 * t)
                        wait(dve, result_done, 2 * (t - 1))
                        nc.vector.tensor_tensor(x_plus_x1[:, :, :], x1[:, :, :], x_res[:, :, :],
                                                ALU.add).then_inc(sum_done, 1)
                    if ahead and p == 6:
                        gain(t + 1, 0, 0, EXTRA, xT1_done, xn1, xn1_lo_done, gained1)
                        add_shift(t + 1, 0, 1, xn1, gained1, xn1_done)
                    if mlp and p >= LAG:
                        silu(t - 1, p - LAG)
                        hidden(t - 1, p - LAG)
                    if ahead and p == 5:
                        scale_rows(t + 1, x_in, inv1, inv1_done, x_scaled1, xT1_done, scaled1)
                if attend:
                    reciprocals(t, PAIRS - 2)
                    normalise(t, PAIRS - 2)
                if ahead:
                    low_k(t + 1)
                if attend:
                    reciprocals(t, PAIRS - 1)
                    normalise(t, PAIRS - 1)
                if ahead:
                    low_q(t + 1, 0)
                if attend:
                    for half in range(2):
                        dve.wait_ge(attT_hi_done, 2 * t + half + 1)
                        wait(dve, proj_mm, 2 * t)
                        cols = slice(half * 256, half * 256 + 256)
                        for head in range(2):
                            last = nc.vector.tensor_tensor(
                                attT_lo[:, head, cols].rearrange("p (b q) -> p b q", q=L),
                                ps[:, OUT + half, :].rearrange("p (b h q) -> p b h q", h=2, q=L)[:, :, head, :],
                                attT_hi[:, head, cols].bitcast(F32).rearrange("p (b q) -> p b q", q=L), ALU.subtract)
                        last.then_inc(attT_lo_done, 1)
                if ahead:
                    low_q(t + 1, 1)
                    for half in range(2):
                        odd_values(t + 1, half)
                if attend:
                    wait(dve, sum_done, t)
                    wait(dve, ms2_done, t)
                    if isinstance(t, int) and t == 0:
                        dve.wait_ge(mlp_w_split, 3)
                    dve.wait_ge(x_res_done, t + 1)
                    for half in range(2):
                        dve.wait_ge(proj_mm, 2 * t + half + 1)
                        nc.vector.tensor_tensor(x1[:, 2 * half:2 * half + 2, :],
                                                ps[:, OUT + half, :].rearrange("p (k n) -> p k n", k=2),
                                                x_res[:, 2 * half:2 * half + 2, :], ALU.add).then_inc(x1_done, 1)
                if mlp:
                    silu(t - 1, CHUNKS - 2)
                    hidden(t - 1, CHUNKS - 2)
                if attend:
                    scale_rows(t, x1, inv2, inv2_done, x_scaled2, xT2_done, scaled2)

            over_tiles(dve, iteration)

        @block.tensor
        def _(pe):
            def three_passes(dst, a_hi, a_lo, b_hi, b_lo, first, last, skip=False):
                nc.tensor.matmul(dst, a_hi, b_hi, start=first, stop=False, skip_group_check=skip)
                nc.tensor.matmul(dst, a_hi, b_lo, start=False, stop=False, skip_group_check=skip)
                return nc.tensor.matmul(dst, a_lo, b_hi, start=False, stop=last, skip_group_check=skip)

            def transpose_norm1(u, c, bank):
                pe.wait_ge(scaled1, u + 1)
                for k in range(BLK):
                    last = nc.tensor.transpose(ps[:, bank, k * P:(k + 1) * P],
                                               x_scaled1[:, k, c * P:(c + 1) * P], ident)
                last.then_inc(xT1_done, 1)

            def transpose_norm2(u, c):
                pe.wait_ge(scaled2, u + 1)
                wait(pe, gained2, CH * u + c)
                for k in range(BLK):
                    last = nc.tensor.transpose(ps[:, EXTRA, k * P:(k + 1) * P],
                                               x_scaled2[:, k, c * P:(c + 1) * P], ident)
                last.then_inc(xT2_done, 1)

            def channel_major(m, c, dst):
                for i in range(CH):
                    w = slice(c * P, (c + 1) * P)
                    last = three_passes(dst, att_w_hi[:, m, i, w], att_w_lo[:, m, i, w],
                                        xn1_hi[:, i, :], xn1_lo[:, i, :], i == 0, i == CH - 1)
                return last

            def project_k(u):
                pe.wait_ge(xn1_lo_done, CH * u + CH)
                wait(pe, shift_done, PAIRS * u)
                wait(pe, exp_done, PAIRS * u)
                for c in range(CH):
                    channel_major(1, c, ps[:, SCORE + c, :]).then_inc(k_mm, 1)

            def project_q(u, c):
                wait(pe, h_done, CHUNKS * (u - 1) - LAG)
                channel_major(0, c, ps[:, GATE + c, :]).then_inc(q_mm, 1)

            def project_v(u, half):
                pe.wait_ge(k_lo_done, CH * u + half + 1)
                for k in (2 * half, 2 * half + 1):
                    tok = slice(k * P, (k + 1) * P)
                    for i in range(CH):
                        last = three_passes(ps[:, SCORE + k // 2, (k % 2) * D:(k % 2) * D + D],
                                            xn1_hi[:, i, tok], xn1_lo[:, i, tok],
                                            att_w_hi[:, 2, i, :], att_w_lo[:, 2, i, :], i == 0, i == CH - 1)
                last.then_inc(v_mm, 1)

            def scores(t, p):
                r, c = p // CH, p % CH
                if c == 0:
                    pe.wait_ge(stacked[r % 2], FILL * (2 * t + r // 2 + 1))
                if p == 0:
                    pe.wait_ge(v_even, 2 * t + 1)
                    pe.wait_ge(v_odd, 2 * t + 1)
                wait(pe, shift_done, PAIRS * t + p)
                for b in range(SEQS):
                    tok = slice(b * L, (b + 1) * L)
                    last = nc.tensor.matmul(ps[:, SCORE, tok], q_stack[:, r % 2, c, b, :], k_stack[:, r % 2, c, tok],
                                            start=True, stop=True)
                last.then_inc(score_mm, 1)

            def transpose_shifted(t, p):
                pe.wait_ge(shift_done, PAIRS * t + p + 1)
                if p == 0:
                    pe.wait_ge(v_even, 2 * t + 2)
                    pe.wait_ge(v_odd, 2 * t + 2)
                wait(pe, exp_done, PAIRS * t + p)
                for k in range(BLK):
                    last = nc.tensor.transpose(ps[:, TRANS, k * P:(k + 1) * P], shifted[:, k * P:(k + 1) * P], ident)
                last.then_inc(shiftT_done, 1)

            def probs_values(t, p):
                pe.wait_ge(exp_done, PAIRS * t + p + 1)
                if p == 0:
                    wait(pe, x1_done, 2 * t)
                wait(pe, att_done, PAIRS * t + p)
                for k in range(BLK):
                    last = nc.tensor.matmul(ps[:, OUT, k * VW:(k + 1) * VW], probsT[:, p % 2, k * P:(k + 1) * P],
                                            values[:, k, pair_of(p), :], start=True, stop=True)
                last.then_inc(pv_mm, 1)

            def gate_hidden(u, j):
                wait(pe, h_done, CHUNKS * u + j)
                w = slice(j * P, (j + 1) * P)
                for bank, hi, lo, done in ((GATE, gate_w_hi, gate_w_lo, gate_mm), (HIDDEN, hid_w_hi, hid_w_lo, hid_mm)):
                    for i in range(CH):
                        if j == 0 and bank == GATE:
                            pe.wait_ge(xn2_hi_done, CH * u + i + 1)
                        nc.tensor.matmul(ps[:, bank, :], hi[:, i, w], xn2_hi[:, i, :], start=i == 0, stop=False)
                        nc.tensor.matmul(ps[:, bank, :], lo[:, i, w], xn2_hi[:, i, :], start=False, stop=False)
                    for i in range(CH):
                        if j == 0 and bank == GATE:
                            pe.wait_ge(xn2_lo_done, CH * u + i + 1)
                        last = nc.tensor.matmul(ps[:, bank, :], hi[:, i, w], xn2_lo[:, i, :], start=False,
                                                stop=i == CH - 1)
                    last.then_inc(done, 1)

            def down(u, j):
                pe.wait_ge(h_lo_done, CHUNKS * u + j + 1)
                if j == 0:
                    wait(pe, result_done, 2 * u)
                for k in range(BLK):
                    tok = slice(k * P, (k + 1) * P)
                    last = three_passes(ps[:, Y + k // 2, (k % 2) * D:(k % 2) * D + D],
                                        h_hi[:, j % 2, tok], h_lo[:, j % 2, tok],
                                        out_w_hi[:, j, :], out_w_lo[:, j, :],
                                        j == 0 and k % 2 == 0, j == CHUNKS - 1, skip=True)
                last.then_inc(down_mm, 1)

            pe.wait_ge(mod_in, 9 * 16)
            for m in range(4):
                for c in range(CH):
                    at = ((m % 2) * CH + c) * B
                    nc.tensor.matmul(ps[:, Y + m // 2, at:at + B], mod_w[:, m, c * P:(c + 1) * P], cond_sb[:, :],
                                     start=True, stop=True).then_inc(mod_mm, 1)
            pe.wait_ge(consts_in, 16)
            for c in range(CH):
                transpose_norm1(0, c, SCORE + c)
            pe.wait_ge(att_w_split, 1)
            project_k(0)
            for c in range(CH):
                project_q(0, c)
            for half in range(2):
                project_v(0, half)

            def iteration(t, attend, mlp, finish, ahead):
                for p in range(PAIRS):
                    if attend:
                        scores(t, p)
                    if mlp and p < CH:
                        transpose_norm2(t - 1, p)
                    if ahead and p == 6:
                        transpose_norm1(t + 1, 0, EXTRA)
                    if finish and p == 0:
                        gate_hidden(t - 2, CHUNKS - 1)
                    if finish and p == 1:
                        down(t - 2, CHUNKS - 2)
                    if finish and p == 2:
                        down(t - 2, CHUNKS - 1)
                    if attend and 1 <= p <= LAG:
                        probs_values(t, p - 1)
                    if mlp and p >= LAG:
                        if isinstance(t, int) and t == 1 and p == LAG:
                            pe.wait_ge(mlp_w_split, 3)
                        gate_hidden(t - 1, p - LAG)
                    if attend:
                        transpose_shifted(t, p)
                    if mlp and p > LAG:
                        down(t - 1, p - LAG - 1)
                    if attend and p > LAG:
                        probs_values(t, p - 1)
                    if ahead and p == 6:
                        pe.wait_ge(gained1, CH * t + CH + 1)
                        transpose_norm1(t + 1, 1, EXTRA)
                if ahead:
                    project_k(t + 1)
                if attend:
                    probs_values(t, PAIRS - 1)
                if ahead:
                    project_q(t + 1, 0)
                if attend:
                    pe.wait_ge(att_done, PAIRS * t + PAIRS)
                    if ahead:
                        pe.wait_ge(gained1, CH * t + 2 * CH)
                    for half in range(2):
                        for b in range(SEQS // 2):
                            last = nc.tensor.transpose(
                                ps[:, OUT + half, b * P:(b + 1) * P],
                                att[:, half * 4 + b, :, :].rearrange("p n d -> p (n d)"), ident)
                        last.then_inc(attT_mm, 1)
                if ahead:
                    project_q(t + 1, 1)
                    for half in range(2):
                        project_v(t + 1, half)
                if attend:
                    for k in range(BLK):
                        tok = slice(k * P, (k + 1) * P)
                        pe.wait_ge(attT_lo_done, 2 * t + k // 2 + 1)
                        for head in range(2):
                            last = three_passes(ps[:, OUT + k // 2, (k % 2) * D:(k % 2) * D + D],
                                                attT_hi[:, head, tok], attT_lo[:, head, tok],
                                                att_w_hi[:, 3, head, :], att_w_lo[:, 3, head, :], head == 0, head == 1)
                        if k % 2:
                            last.then_inc(proj_mm, 1)
                if mlp:
                    if ahead:
                        pe.wait_ge(q_lo_done, CH * t + 2 * CH)
                    gate_hidden(t - 1, CHUNKS - 2)
                    down(t - 1, CHUNKS - 3)

            over_tiles(pe, iteration)


_NAMES = ["x", "condT", "WqT", "WkT", "WvT", "WoT", "g1wT", "g1b", "b1wT", "b1b", "g2wT", "g2b", "b2wT", "b2b",
          "gateT", "hidT", "outT", "consts"]


def kernel(**inputs):
    import numpy as np
    import concourse.bacc as bacc
    from concourse.bass_utils import run_bass_kernel_spmd

    a = {k.removeprefix("L0_cond_"): np.asarray(v) for k, v in inputs.items()}
    columns = lambda v: v.reshape(CH, P).T
    wo_rows = a["Wo"].T.reshape(PAIRS, 2, DH, D).transpose(1, 0, 2, 3).reshape(D, D)
    head_of_row = (np.arange(P) // DH) % 2
    consts = np.concatenate([np.eye(P), np.stack([(head_of_row == n) * 0.25 for n in range(2)], 1)], 1).astype(np.float32)
    laid = {
        "x": a["x"], "condT": a["cond_256"].T, "WqT": a["Wq"].T, "WkT": a["Wk"].T, "WvT": a["Wv"].T, "WoT": wo_rows,
        "g1wT": a["g1w"].T, "g1b": columns(a["g1b"]), "b1wT": a["b1w"].T, "b1b": columns(a["b1b"]),
        "g2wT": a["g2w"].T, "g2b": columns(a["g2b"]), "b2wT": a["b2w"].T, "b2b": columns(a["b2b"]),
        "gateT": a["gate_w"].T, "hidT": a["hid_w"].T, "outT": a["out_w"].T, "consts": consts,
    }
    nc = bacc.Bacc("TRN2", target_bir_lowering=False, num_devices=1)
    arrays, args = {}, []
    for name in _NAMES:
        v = np.ascontiguousarray(laid[name])
        arrays[f"in_{name}"] = v
        args.append(nc.dram_tensor(f"in_{name}", v.shape, mybir.dt.from_np(v.dtype), kind="ExternalInput").ap())
    args.append(nc.dram_tensor("out_0", (B, L, D), F32, kind="ExternalOutput").ap())
    conditioned_block(nc, *args)
    r = run_bass_kernel_spmd(nc, [arrays], core_ids=[0])
    return r.results[0]["out_0"]
```

```python
from contextlib import ExitStack

import concourse.bass as bass
from concourse import mybir

ALU = mybir.AluOpType
ACT = mybir.ActivationFunctionType
AX_X = mybir.AxisListType.X
F32 = mybir.dt.float32
F32R = mybir.dt.float32r

P = 128
B, L, D = 128, 64, 256
DT = 64
HEADS, DH = 16, 16
HID = 4 * D
EPS = 1e-6
SEQS = 8
TOK = SEQS * L
TILES = B // SEQS
BLK = TOK // P
CH = D // P
PAIRS = HEADS // 2
ROWS = 2 * DH
CHUNKS = HID // P
LAG = 2
VW = 2 * ROWS + 2

STACK = 3
ROUNDS = PAIRS // CH
FILL_K, FILL_S0, FILL_S1, FILL_STEP = 8, 10, 6, 4
FILL = 16 * 2 * STACK

GATE, HIDDEN, Y, SCORE, TRANS, OUT, EXTRA = 0, 1, 2, 4, 5, 6, 7


def conditioned_block(nc, x, condT, modT, attT, gateT, hidT, outT, consts, out):
    x_t = x.rearrange("(t k s) l c -> t (s l) k c", k=BLK, s=P // L)
    out_t = out.rearrange("(t k s) l c -> t (s l) k c", k=BLK, s=P // L)

    with ExitStack() as ctx:
        def sb(name, shape, dt=F32):
            return ctx.enter_context(nc.sbuf_tensor(name, shape, dt))

        def sem(name):
            return ctx.enter_context(nc.semaphore(name))

        ps = ctx.enter_context(nc.psum_tensor("ps", [P, 8, 512], F32))

        consts_sb = sb("consts_sb", [P, P + 2 + 4 * CH])
        ident = consts_sb[:, 0:P]
        head_mask = consts_sb[:, P:P + 2]
        mod_bias = consts_sb[:, P + 2:]
        shared = sb("shared", [P, 4, BLK * D])
        raw = shared[:, :, :].rearrange("p (a b) n -> p a (b n)", a=2)
        att_w_hi = sb("att_w_hi", [P, 4, CH, D], F32R)
        att_w_lo = sb("att_w_lo", [P, 4, CH, D], F32R)
        gate_w_hi = sb("gate_w_hi", [P, CH, HID], F32R)
        gate_w_lo = sb("gate_w_lo", [P, CH, HID], F32R)
        hid_w_hi = sb("hid_w_hi", [P, CH, HID], F32R)
        hid_w_lo = sb("hid_w_lo", [P, CH, HID], F32R)
        out_w_hi = sb("out_w_hi", [P, CHUNKS, D], F32R)
        out_w_lo = sb("out_w_lo", [P, CHUNKS, D], F32R)
        cond_sb = sb("cond_sb", [DT, B])
        result = sb("result", [P, BLK, D])
        mod_w = result[0:DT, :, :]
        mod = sb("mod", [P, 4, CH, B])
        eps = sb("eps", [P, BLK])
        minus_half = sb("minus_half", [P, BLK])

        x_in = sb("x_in", [P, BLK, D])
        ms1 = sb("ms1", [P, BLK])
        mse1 = sb("mse1", [P, BLK])
        inv1 = sb("inv1", [P, BLK])
        x_scaled1 = sb("x_scaled1", [P, BLK, D])
        xn1 = sb("xn1", [P, CH, TOK])
        xn1_hi = sb("xn1_hi", [P, CH, TOK], F32R)
        xn1_lo = sb("xn1_lo", [P, CH, TOK], F32R)
        q_hi = sb("q_hi", [P, CH, SEQS, 2, L], F32R)
        q_lo = sb("q_lo", [P, CH, SEQS, 2, L], F32R)
        k_hi = sb("k_hi", [P, CH, TOK], F32R)
        k_lo = sb("k_lo", [P, CH, TOK], F32R)
        q_stack = sb("q_stack", [STACK * ROWS, 2, CH, SEQS, 2 * L], F32R)
        k_stack = sb("k_stack", [STACK * ROWS, 2, CH, TOK], F32R)
        values = sb("values", [P, BLK, PAIRS, VW])
        row_max = sb("row_max", [P, 2, SEQS])
        shifted = sb("shifted", [P, TOK])
        probsT = sb("probsT", [P, 2, TOK])
        recip = sb("recip", [P, SEQS])
        att = sb("att", [P, SEQS, PAIRS, DH])
        attT_hi = sb("attT_hi", [P, 2, TOK], F32R)
        attT_lo = sb("attT_lo", [P, 2, TOK], F32R)
        x_res = sb("x_res", [P, BLK, D])
        x_plus_x1 = sb("x_plus_x1", [P, BLK, D])
        x1 = shared[:, 2, :].rearrange("p (k n) -> p k n", k=BLK)
        ms2 = sb("ms2", [P, BLK])
        mse2 = sb("mse2", [P, BLK])
        inv2 = sb("inv2", [P, BLK])
        x_scaled2 = shared[:, 0, :].rearrange("p (k n) -> p k n", k=BLK)
        xn2 = shared[:, 1, :].rearrange("p (c n) -> p c n", c=CH)
        xn2_hi = sb("xn2_hi", [P, CH, TOK], F32R)
        xn2_lo = sb("xn2_lo", [P, CH, TOK], F32R)
        act_g = shared[:, 3, 0:TOK]
        h = shared[:, 3, TOK:2 * TOK]
        h_hi = sb("h_hi", [P, 2, TOK], F32R)
        h_lo = sb("h_lo", [P, 2, TOK], F32R)

        consts_in, mod_in, att_w_in, gate_w_in, hid_w_in, out_w_in = map(
            sem, ["consts_in", "mod_in", "att_w_in", "gate_w_in", "hid_w_in", "out_w_in"])
        w_hi_done, w_split = sem("w_hi_done"), sem("w_split")
        mod_mm, mod_done, table_loaded, powers_set, values_zeroed, values_set = map(
            sem, ["mod_mm", "mod_done", "table_loaded", "powers_set", "values_zeroed", "values_set"])
        x_loaded, x_res_done, stored = sem("x_loaded"), sem("x_res_done"), sem("stored")
        ms1_done, mse1_done, inv1_done, scaled1 = map(sem, ["ms1_done", "mse1_done", "inv1_done", "scaled1"])
        xT1_done, gained1, xn1_done, xn1_hi_done, xn1_lo_done = map(
            sem, ["xT1_done", "gained1", "xn1_done", "xn1_hi_done", "xn1_lo_done"])
        q_mm, q_hi_done, q_lo_done, k_mm, k_hi_done, k_lo_done, v_mm, v_even, v_odd = map(
            sem, ["q_mm", "q_hi_done", "q_lo_done", "k_mm", "k_hi_done", "k_lo_done", "v_mm", "v_even", "v_odd"])
        stacked = [sem("stacked_even"), sem("stacked_odd")]
        score_mm, max_done, shift_done, shiftT_done, exp_done, pv_mm, recip_done, att_done = map(
            sem, ["score_mm", "max_done", "shift_done", "shiftT_done", "exp_done", "pv_mm", "recip_done", "att_done"])
        attT_mm, attT_hi_done, attT_lo_done, proj_mm, x1_done, sum_done = map(
            sem, ["attT_mm", "attT_hi_done", "attT_lo_done", "proj_mm", "x1_done", "sum_done"])
        ms2_done, mse2_done, inv2_done, scaled2 = map(sem, ["ms2_done", "mse2_done", "inv2_done", "scaled2"])
        xT2_done, gained2, xn2_done, xn2_hi_done, xn2_lo_done = map(
            sem, ["xT2_done", "gained2", "xn2_done", "xn2_hi_done", "xn2_lo_done"])
        gate_mm, hid_mm, tanh_done, silu_done, h_done, h_hi_done, h_lo_done, down_mm, result_done = map(
            sem, ["gate_mm", "hid_mm", "tanh_done", "silu_done", "h_done", "h_hi_done", "h_lo_done",
                  "down_mm", "result_done"])

        def wait(eng, semaphore, count):
            if not isinstance(count, int) or count > 0:
                eng.wait_ge(semaphore, count)

        def over_tiles(eng, iteration):
            iteration(0, attend=True, mlp=False, finish=False, ahead=True)
            iteration(1, attend=True, mlp=True, finish=False, ahead=True)
            with eng.Fori(2, TILES - 1) as t:
                iteration(t, attend=True, mlp=True, finish=True, ahead=True)
            iteration(TILES - 1, attend=True, mlp=True, finish=True, ahead=False)
            iteration(TILES, attend=False, mlp=True, finish=True, ahead=False)
            iteration(TILES + 1, attend=False, mlp=False, finish=True, ahead=False)

        def pair_of(p):
            return (p % CH) * (PAIRS // CH) + p // CH

        def alone(t):
            return isinstance(t, int) and t == 0

        def step_ahead(t, p):
            return p - 2 if alone(t) else p

        def score_bank(t, p):
            return GATE if alone(t) and p % 2 else SCORE

        block = ctx.enter_context(nc.Block())

        @block.sync
        def _(sp):
            sp.dma_start(x_in[:, :, :], x_t[0]).then_inc(x_loaded, 16)
            sp.dma_start(mod_w, modT).then_inc(mod_in, 16)
            sp.dma_start(raw[:, 0, :], attT).then_inc(att_w_in, 16)
            sp.dma_start(raw[:, 1, :].rearrange("p (c n) -> p c n", c=CH),
                         gateT.rearrange("(c p) n -> p c n", p=P)).then_inc(gate_w_in, 16)
            sp.wait_ge(w_split, 2)
            sp.dma_start(raw[:, 0, :].rearrange("p (c n) -> p c n", c=CH),
                         hidT.rearrange("(c p) n -> p c n", p=P)).then_inc(hid_w_in, 16)

            def stack_k(u, r):
                if r < 2:
                    sp.wait_ge(k_lo_done, CH * u + CH)
                wait(sp, score_mm, PAIRS * u + CH * (r - 1))
                for s, k in enumerate((k_hi, k_lo, k_hi)):
                    sp.dma_start(k_stack[s * ROWS:(s + 1) * ROWS, r % 2, :, :].bitcast(F32),
                                 k[r * ROWS:(r + 1) * ROWS, :, :].bitcast(F32)).then_inc(stacked[r % 2], 16)

            def stack_q(u, r):
                if r < 2:
                    sp.wait_ge(q_lo_done, CH * u + CH)
                for s, q in enumerate((q_hi, q_hi, q_lo)):
                    sp.dma_start(q_stack[s * ROWS:(s + 1) * ROWS, r % 2, :, :, :].rearrange(
                                     "p c b n -> p c (b n)").bitcast(F32),
                                 q[r * ROWS:(r + 1) * ROWS, :, :, :, :].rearrange("p c b h n -> p c (b h n)").bitcast(F32)
                                 ).then_inc(stacked[r % 2], 16)

            def stack_first_rounds(u):
                for r in range(2):
                    stack_k(u, r)
                for r in range(2):
                    stack_q(u, r)

            stack_first_rounds(0)
            sp.wait_ge(w_split, 3)
            sp.dma_start(raw[:, 1, :].rearrange("p (j n) -> p j n", j=CHUNKS),
                         outT.rearrange("(j p) n -> p j n", p=P)).then_inc(out_w_in, 16)

            def iteration(t, attend, mlp, finish, ahead):
                if attend:
                    stack_k(t, 2)
                    stack_q(t, 2)
                if finish and (attend or mlp):
                    sp.wait_ge(result_done, 2 * (t - 1))
                    sp.dma_start(out_t[t - 2], result[:, :, :]).then_inc(stored, 16)
                if finish and not (attend or mlp):
                    for half in range(2):
                        blocks = slice(2 * half, 2 * half + 2)
                        sp.wait_ge(result_done, 2 * (t - 1) - 1 + half)
                        sp.dma_start(out_t[t - 2, :, blocks, :], result[:, blocks, :]).then_inc(stored, 16)
                if ahead:
                    sp.wait_ge(x_res_done, t + 1)
                    sp.wait_ge(scaled1, t + 1)
                    sp.dma_start(x_in[:, :, :], x_t[t + 1]).then_inc(x_loaded, 16)
                if attend:
                    stack_k(t, 3)
                    stack_q(t, 3)
                if ahead:
                    stack_first_rounds(t + 1)

            over_tiles(sp, iteration)
            sp.wait_ge(stored, 16 * (TILES + 1))

        @block.gpsimd
        def _(pool):
            pool.memset(eps[:, :], EPS).then_inc(powers_set, 1)
            pool.memset(minus_half[:, :], -0.5).then_inc(powers_set, 1)
            pool.memset(values[:, :, :, :], 0.0).then_inc(values_zeroed, 1)
            pool.wait_ge(values_zeroed, 1)
            pool.memset(values[0:L, :, :, VW - 2:VW - 1], 1.0).then_inc(values_set, 1)
            pool.memset(values[L:P, :, :, VW - 1:VW], 1.0).then_inc(values_set, 1)
            pool.wait_ge(powers_set, 2)
            pool.wait_ge(values_set, 2)

            def inverse_rms(u, ms, ms_done, mse, mse_done, inv, inv_done, scaled):
                pool.wait_ge(ms_done, u + 1)
                nc.gpsimd.tensor_tensor(mse[:, :], ms[:, :], eps[:, :], ALU.add).then_inc(mse_done, 1)
                pool.wait_ge(mse_done, u + 1)
                wait(pool, scaled, u)
                nc.gpsimd.tensor_tensor(inv[:, :], mse[:, :], minus_half[:, :], ALU.pow).then_inc(inv_done, 1)

            def low_norm(u, c, xn, xn_hi, xn_lo, hi_done, lo_done, used, uses):
                pool.wait_ge(hi_done, CH * u + c + 1)
                wait(pool, used, uses)
                nc.gpsimd.tensor_tensor(xn_lo[:, c, :], xn[:, c, :], xn_hi[:, c, :].bitcast(F32),
                                        ALU.subtract).then_inc(lo_done, 1)

            def low_norm1(u, c):
                low_norm(u, c, xn1, xn1_hi, xn1_lo, xn1_hi_done, xn1_lo_done, v_mm, 2 * u)

            def low_norm2(u, c):
                low_norm(u, c, xn2, xn2_hi, xn2_lo, xn2_hi_done, xn2_lo_done, hid_mm, CHUNKS * u)

            def low_hidden(u, j):
                pool.wait_ge(h_hi_done, CHUNKS * u + j + 1)
                wait(pool, down_mm, CHUNKS * u + j - 1)
                nc.gpsimd.tensor_tensor(h_lo[:, j % 2, :], h[:, :], h_hi[:, j % 2, :].bitcast(F32),
                                        ALU.subtract).then_inc(h_lo_done, 1)

            inverse_rms(0, ms1, ms1_done, mse1, mse1_done, inv1, inv1_done, scaled1)

            def low_weights(n, lo, hi, piece):
                pool.wait_ge(w_hi_done, n + 2)
                nc.gpsimd.tensor_tensor(lo, raw[:, piece, :], hi.bitcast(F32), ALU.subtract).then_inc(w_split, 1)

            for part in range(2):
                pool.wait_ge(w_hi_done, part + 1)
                nc.gpsimd.tensor_tensor(att_w_lo[:, 2 * part:2 * part + 2, :, :].rearrange("p m c n -> p (m c n)"),
                                        raw[:, 0, part * HID:(part + 1) * HID],
                                        att_w_hi[:, 2 * part:2 * part + 2, :, :].rearrange(
                                            "p m c n -> p (m c n)").bitcast(F32), ALU.subtract).then_inc(w_split, 1)
            low_weights(1, gate_w_lo[:, :, :].rearrange("p c n -> p (c n)"),
                        gate_w_hi[:, :, :].rearrange("p c n -> p (c n)"), 1)

            def iteration(t, attend, mlp, finish, ahead):
                for p in range(PAIRS):
                    if mlp and p == 1:
                        low_norm2(t - 1, 0)
                    if finish and p == 1:
                        low_hidden(t - 2, CHUNKS - 1)
                    if mlp and p == 1:
                        low_norm2(t - 1, 1)
                    if ahead and p == step_ahead(t, 7):
                        low_norm1(t + 1, 1)
                    if mlp and p >= LAG:
                        low_hidden(t - 1, p - LAG)
                    if ahead and p == step_ahead(t, 6):
                        low_norm1(t + 1, 0)
                    if ahead and p == step_ahead(t, 4):
                        inverse_rms(t + 1, ms1, ms1_done, mse1, mse1_done, inv1, inv1_done, scaled1)
                    if alone(t) and p == 2:
                        low_weights(2, hid_w_lo[:, :, :].rearrange("p c n -> p (c n)"),
                                    hid_w_hi[:, :, :].rearrange("p c n -> p (c n)"), 0)
                    if alone(t) and p == 5:
                        low_weights(3, out_w_lo[:, :, :].rearrange("p j n -> p (j n)"),
                                    out_w_hi[:, :, :].rearrange("p j n -> p (j n)"), 1)
                if mlp and not ahead:
                    low_hidden(t - 1, CHUNKS - 2)
                if attend:
                    inverse_rms(t, ms2, ms2_done, mse2, mse2_done, inv2, inv2_done, scaled2)
                if mlp and ahead:
                    low_hidden(t - 1, CHUNKS - 2)

            over_tiles(pool, iteration)

        @block.scalar
        def _(act):
            act.dma_start(cond_sb[:, :], condT).then_inc(mod_in, 16)
            act.dma_start(consts_sb[:, :], consts).then_inc(consts_in, 16)
            act.wait_ge(powers_set, 2)
            nc.scalar.activation(ms1[:, :], minus_half[:, :], ACT.Square).then_inc(table_loaded, 1)
            act.wait_ge(table_loaded, 1)

            def high_weights(n, landed, count, hi, piece):
                act.wait_ge(landed, count)
                nc.scalar.copy(hi, raw[:, piece, :]).then_inc(w_hi_done, 1)

            def mean_squares(u, src, ready, counts, squares, transposed, ms, ms_done):
                wait(act, transposed, CH * u)
                for k in range(BLK):
                    if k % 2 == 0:
                        act.wait_ge(ready, counts[k // 2])
                    last = nc.scalar.activation(squares[:, k, :], src[:, k, :], ACT.Square, scale=float(D) ** -0.5,
                                                accum_out=ms[:, k:k + 1])
                last.then_inc(ms_done, 1)

            def high_norm1(u, c):
                act.wait_ge(xn1_done, CH * u + c + 1)
                wait(act, v_mm, 2 * u)
                nc.scalar.copy(xn1_hi[:, c, :], xn1[:, c, :]).then_inc(xn1_hi_done, 1)

            def high_norm2(u, c):
                act.wait_ge(xn2_done, CH * u + c + 1)
                wait(act, hid_mm, CHUNKS * u)
                nc.scalar.copy(xn2_hi[:, c, :], xn2[:, c, :]).then_inc(xn2_hi_done, 1)

            def high_k(u):
                for c in range(CH):
                    act.wait_ge(k_mm, CH * u + c + 1)
                    if c == 0:
                        wait(act, stacked[0], 2 * FILL * u)
                        wait(act, stacked[1], 2 * FILL * u)
                    nc.scalar.copy(k_hi[:, c, :], ps[:, SCORE + c, :]).then_inc(k_hi_done, 1)

            def high_q(u, c):
                act.wait_ge(q_mm, CH * u + c + 1)
                for head in range(2):
                    last = nc.scalar.activation(q_hi[:, c, :, head, :],
                                                ps[:, GATE + c, :].rearrange("p (b q) -> p b q", q=L), ACT.Copy,
                                                scale=head_mask[:, head:head + 1])
                last.then_inc(q_hi_done, 1)

            def even_values(u, half):
                act.wait_ge(v_mm, 2 * u + half + 1)
                wait(act, pv_mm, PAIRS * u)
                if isinstance(u, int) and u == 0:
                    act.wait_ge(values_set, 2)
                nc.scalar.copy(values[0:L, 2 * half:2 * half + 2, :, 0:ROWS],
                               ps[0:L, SCORE + half, :].rearrange("p (k n d) -> p k n d", k=2, d=ROWS)
                               ).then_inc(v_even, 1)

            def tanh(u, j):
                act.wait_ge(gate_mm, CHUNKS * u + j + 1)
                wait(act, h_done, CHUNKS * u + j)
                nc.scalar.activation(act_g[:, :], ps[:, GATE, :], ACT.Tanh, scale=0.5).then_inc(tanh_done, 1)

            def high_hidden(u, j):
                act.wait_ge(h_done, CHUNKS * u + j + 1)
                wait(act, down_mm, CHUNKS * u + j - 1)
                nc.scalar.copy(h_hi[:, j % 2, :], h[:, :]).then_inc(h_hi_done, 1)

            def exp(t, p):
                act.wait_ge(shiftT_done, PAIRS * t + p + 1)
                wait(act, pv_mm, PAIRS * t + p - 1)
                nc.scalar.activation(probsT[:, p % 2, :], ps[:, TRANS, :], ACT.Exp).then_inc(exp_done, 1)

            mean_squares(0, x_in, x_loaded, (16, 16), x_scaled1, xT1_done, ms1, ms1_done)
            act.wait_ge(att_w_in, 16)
            for part in range(2):
                nc.scalar.copy(att_w_hi[:, 2 * part:2 * part + 2, :, :].rearrange("p m c n -> p (m c n)"),
                               raw[:, 0, part * HID:(part + 1) * HID]).then_inc(w_hi_done, 1)
            act.wait_ge(consts_in, 16)
            for c in range(CH):
                high_norm1(0, c)
            high_weights(1, gate_w_in, 16, gate_w_hi[:, :, :].rearrange("p c n -> p (c n)"), 1)
            high_k(0)
            for c in range(CH):
                high_q(0, c)
            for half in range(2):
                even_values(0, half)

            def iteration(t, attend, mlp, finish, ahead):
                for p in range(PAIRS):
                    if ahead and p == step_ahead(t, 7):
                        high_norm1(t + 1, 1)
                    if mlp and p >= LAG:
                        tanh(t - 1, p - LAG)
                    if finish and p == 0:
                        tanh(t - 2, CHUNKS - 1)
                    if attend:
                        exp(t, p)
                    if not mlp and attend and p == 1:
                        high_weights(2, hid_w_in, 16, hid_w_hi[:, :, :].rearrange("p c n -> p (c n)"), 0)
                    if not mlp and attend and p == 3:
                        high_weights(3, out_w_in, 16, out_w_hi[:, :, :].rearrange("p j n -> p (j n)"), 1)
                    if mlp and p == 0:
                        high_norm2(t - 1, 0)
                    if finish and p == 0:
                        high_hidden(t - 2, CHUNKS - 1)
                    if mlp and p == 0:
                        high_norm2(t - 1, 1)
                    if ahead and p == step_ahead(t, 6):
                        high_norm1(t + 1, 0)
                    if mlp and p >= LAG:
                        high_hidden(t - 1, p - LAG)
                    if attend and p == (0 if alone(t) else 3):
                        wait(act, sum_done, t)
                        act.wait_ge(x_loaded, 16 * t + 16)
                        nc.scalar.copy(x_res[:, :, :], x_in[:, :, :]).then_inc(x_res_done, 1)
                    if ahead and p == step_ahead(t, 4):
                        mean_squares(t + 1, x_in, x_loaded, (16 * t + 32, 16 * t + 32), x_scaled1, xT1_done,
                                     ms1, ms1_done)
                if mlp and not ahead:
                    tanh(t - 1, CHUNKS - 2)
                    high_hidden(t - 1, CHUNKS - 2)
                if ahead:
                    high_k(t + 1)
                    high_q(t + 1, 0)
                if attend:
                    for half in range(2):
                        act.wait_ge(attT_mm, 2 * t + half + 1)
                        wait(act, proj_mm, 2 * t)
                        nc.scalar.copy(
                            attT_hi[:, :, half * 256:half * 256 + 256].rearrange("p h (b q) -> p b h q", q=L),
                            ps[:, OUT + half, :].rearrange("p (b h q) -> p b h q", h=2, q=L),
                        ).then_inc(attT_hi_done, 1)
                if ahead:
                    high_q(t + 1, 1)
                    for half in range(2):
                        even_values(t + 1, half)
                if attend:
                    mean_squares(t, x1, x1_done, (2 * t + 1, 2 * t + 2), x_scaled2, xT2_done, ms2, ms2_done)
                if mlp and ahead:
                    tanh(t - 1, CHUNKS - 2)
                    high_hidden(t - 1, CHUNKS - 2)

            over_tiles(act, iteration)

        @block.vector
        def _(dve):
            def scale_rows(u, src, inv, inv_done, dst, transposed, scaled):
                dve.wait_ge(inv_done, u + 1)
                wait(dve, transposed, CH * u)
                for k in range(BLK):
                    last = nc.vector.tensor_scalar(dst[:, k, :], src[:, k, :], inv[:, k:k + 1], None, ALU.mult)
                last.then_inc(scaled, 1)

            def of_sequences(m, c, u):
                return mod[:, m, c, bass.ds(u * SEQS, SEQS)].unsqueeze(2).to_broadcast([P, SEQS, L])

            def gain(u, c, m, bank, transposed, xn, xn_lo_done, gained):
                dve.wait_ge(transposed, CH * u + c + 1)
                wait(dve, xn_lo_done, CH * u)
                nc.vector.tensor_tensor(xn[:, c, :].rearrange("p (b q) -> p b q", q=L),
                                        ps[:, bank, :].rearrange("p (b q) -> p b q", q=L),
                                        of_sequences(m, c, u), ALU.mult).then_inc(gained, 1)

            def add_shift(u, c, m, xn, gained, done):
                dve.wait_ge(gained, CH * u + c + 1)
                dst = xn[:, c, :].rearrange("p (b q) -> p b q", q=L)
                nc.vector.tensor_tensor(dst, dst, of_sequences(m, c, u), ALU.add).then_inc(done, 1)

            def low_k(u):
                for c in range(CH):
                    dve.wait_ge(k_hi_done, CH * u + c + 1)
                    nc.vector.tensor_tensor(k_lo[:, c, :], ps[:, SCORE + c, :], k_hi[:, c, :].bitcast(F32),
                                            ALU.subtract).then_inc(k_lo_done, 1)

            def low_q(u, c):
                dve.wait_ge(q_hi_done, CH * u + c + 1)
                for head in range(2):
                    last = nc.vector.scalar_tensor_tensor(
                        q_lo[:, c, :, head, :], ps[:, GATE + c, :].rearrange("p (b q) -> p b q", q=L),
                        head_mask[:, head:head + 1], q_hi[:, c, :, head, :].bitcast(F32),
                        ALU.mult, ALU.subtract)
                last.then_inc(q_lo_done, 1)

            def odd_values(u, half):
                dve.wait_ge(v_mm, 2 * u + half + 1)
                wait(dve, pv_mm, PAIRS * u)
                if isinstance(u, int) and u == 0:
                    dve.wait_ge(values_set, 2)
                nc.vector.tensor_copy(values[L:P, 2 * half:2 * half + 2, :, ROWS:2 * ROWS],
                                      ps[L:P, SCORE + half, :].rearrange("p (k n d) -> p k n d", k=2, d=ROWS)
                                      ).then_inc(v_odd, 1)

            def reciprocals(t, p):
                dve.wait_ge(pv_mm, PAIRS * t + p + 1)
                sums = ps[:, OUT, 0:BLK * VW].rearrange("p (k n) -> p k n", n=VW)[:, :, VW - 2:VW]
                nc.vector.reciprocal(recip[:, :].rearrange("p (k s) -> p k s", s=2), sums).then_inc(recip_done, 1)

            def normalise(t, p):
                dve.wait_ge(recip_done, PAIRS * t + p + 1)
                wait(dve, attT_mm, 2 * t)
                for head in range(2):
                    rows = slice(head * L, head * L + L)
                    own = ps[rows, OUT, 0:BLK * VW].rearrange("p (k n) -> p k n", n=VW)[:, :, 0:2 * ROWS].rearrange(
                        "p k (s h d) -> p k s h d", s=2, h=2)[:, :, :, head, :]
                    last = nc.vector.tensor_tensor(
                        att[rows, :, pair_of(p), :].rearrange("p (k s) d -> p k s d", s=2), own,
                        recip[rows, :].rearrange("p (k s) -> p k s", s=2).unsqueeze(3).to_broadcast([L, BLK, 2, DH]),
                        ALU.mult)
                last.then_inc(att_done, 1)

            def row_maxima(t, p):
                dve.wait_ge(score_mm, PAIRS * t + p + 1)
                nc.vector.tensor_reduce(row_max[:, p % 2, :], ps[:, score_bank(t, p), :].rearrange("p (b k) -> p b k", k=L),
                                        AX_X, ALU.max).then_inc(max_done, 1)

            def shift(t, p):
                dve.wait_ge(max_done, PAIRS * t + p + 1)
                wait(dve, shiftT_done, PAIRS * t + p)
                nc.vector.tensor_tensor(shifted[:, :].rearrange("p (b k) -> p b k", k=L),
                                        ps[:, score_bank(t, p), :].rearrange("p (b k) -> p b k", k=L),
                                        row_max[:, p % 2, :].unsqueeze(2).to_broadcast([P, SEQS, L]),
                                        ALU.subtract).then_inc(shift_done, 1)

            def silu(u, j):
                dve.wait_ge(tanh_done, CHUNKS * u + j + 1)
                nc.vector.scalar_tensor_tensor(act_g[:, :], act_g[:, :], 1.0, ps[:, GATE, :],
                                               ALU.add, ALU.mult).then_inc(silu_done, 1)

            def hidden(u, j):
                dve.wait_ge(silu_done, CHUNKS * u + j + 1)
                dve.wait_ge(hid_mm, CHUNKS * u + j + 1)
                wait(dve, h_lo_done, CHUNKS * u + j)
                nc.vector.scalar_tensor_tensor(h[:, :], act_g[:, :], 0.5, ps[:, HIDDEN, :],
                                               ALU.mult, ALU.mult).then_inc(h_done, 1)

            def results_and_sum(t, mlp, finish):
                if finish:
                    dve.wait_ge(down_mm, CHUNKS * (t - 1))
                    dve.wait_ge(sum_done, t - 1)
                    wait(dve, stored, 16 * (t - 2))
                    for half in range(2):
                        nc.vector.tensor_tensor(result[:, 2 * half:2 * half + 2, :],
                                                ps[:, Y + half, :].rearrange("p (k n) -> p k n", k=2),
                                                x_plus_x1[:, 2 * half:2 * half + 2, :], ALU.add).then_inc(result_done, 1)
                if mlp:
                    dve.wait_ge(x1_done, 2 * t)
                    wait(dve, result_done, 2 * (t - 1))
                    nc.vector.tensor_tensor(x_plus_x1[:, :, :], x1[:, :, :], x_res[:, :, :],
                                            ALU.add).then_inc(sum_done, 1)

            def add_biases(norm):
                dve.wait_ge(consts_in, 16)
                dve.wait_ge(mod_mm, 2 * CH * (norm + 1))
                for m in (2 * norm, 2 * norm + 1):
                    for c in range(CH):
                        at = ((m % 2) * CH + c) * B
                        nc.vector.tensor_scalar(mod[:, m, c, :], ps[:, Y + norm, at:at + B],
                                                mod_bias[:, m * CH + c:m * CH + c + 1], None,
                                                ALU.add).then_inc(mod_done, 1)
                dve.wait_ge(mod_done, 2 * CH * (norm + 1))

            add_biases(0)
            scale_rows(0, x_in, inv1, inv1_done, x_scaled1, xT1_done, scaled1)
            for c in range(CH):
                gain(0, c, 0, SCORE + c, xT1_done, xn1, xn1_lo_done, gained1)
                add_shift(0, c, 1, xn1, gained1, xn1_done)
            for c in range(CH):
                dve.wait_ge(xn1_hi_done, c + 1)
                nc.vector.tensor_tensor(xn1_lo[:, c, :], xn1[:, c, :], xn1_hi[:, c, :].bitcast(F32),
                                        ALU.subtract).then_inc(xn1_lo_done, 1)
            add_biases(1)
            low_k(0)
            for c in range(CH):
                low_q(0, c)
            for half in range(2):
                odd_values(0, half)

            def iteration(t, attend, mlp, finish, ahead):
                for p in range(PAIRS):
                    if ahead and p == step_ahead(t, 7):
                        gain(t + 1, 1, 0, EXTRA, xT1_done, xn1, xn1_lo_done, gained1)
                        add_shift(t + 1, 1, 1, xn1, gained1, xn1_done)
                    if attend and p >= 3 and not alone(t):
                        reciprocals(t, p - 2)
                    if attend:
                        row_maxima(t, p)
                    if attend and p >= 3 and not alone(t):
                        normalise(t, p - 2)
                    if attend:
                        shift(t, p)
                    if alone(t) and p >= 3:
                        reciprocals(t, p - 2)
                        normalise(t, p - 2)
                    if finish and not attend and p == 0:
                        silu(t - 2, CHUNKS - 1)
                        hidden(t - 2, CHUNKS - 1)
                    if mlp and p == 0:
                        gain(t - 1, 0, 2, EXTRA, xT2_done, xn2, xn2_lo_done, gained2)
                        add_shift(t - 1, 0, 3, xn2, gained2, xn2_done)
                    if finish and attend and p == 0:
                        silu(t - 2, CHUNKS - 1)
                        hidden(t - 2, CHUNKS - 1)
                    if mlp and p == 1:
                        gain(t - 1, 1, 2, EXTRA, xT2_done, xn2, xn2_lo_done, gained2)
                        add_shift(t - 1, 1, 3, xn2, gained2, xn2_done)
                    if attend and p == 1:
                        reciprocals(t, 0)
                        normalise(t, 0)
                    if attend and p == 2:
                        results_and_sum(t, mlp, finish)
                    if ahead and p == step_ahead(t, 6):
                        gain(t + 1, 0, 0, EXTRA, xT1_done, xn1, xn1_lo_done, gained1)
                        add_shift(t + 1, 0, 1, xn1, gained1, xn1_done)
                    if mlp and p >= LAG:
                        silu(t - 1, p - LAG)
                        hidden(t - 1, p - LAG)
                    if not attend and p == 2:
                        results_and_sum(t, mlp, finish)
                    if ahead and p == step_ahead(t, 5):
                        scale_rows(t + 1, x_in, inv1, inv1_done, x_scaled1, xT1_done, scaled1)
                if attend:
                    reciprocals(t, PAIRS - 2)
                    normalise(t, PAIRS - 2)
                if mlp and not ahead:
                    silu(t - 1, CHUNKS - 2)
                    hidden(t - 1, CHUNKS - 2)
                if ahead:
                    low_k(t + 1)
                if attend:
                    reciprocals(t, PAIRS - 1)
                    normalise(t, PAIRS - 1)
                if ahead:
                    low_q(t + 1, 0)
                if attend:
                    for half in range(2):
                        dve.wait_ge(attT_hi_done, 2 * t + half + 1)
                        wait(dve, proj_mm, 2 * t)
                        cols = slice(half * 256, half * 256 + 256)
                        for head in range(2):
                            last = nc.vector.tensor_tensor(
                                attT_lo[:, head, cols].rearrange("p (b q) -> p b q", q=L),
                                ps[:, OUT + half, :].rearrange("p (b h q) -> p b h q", h=2, q=L)[:, :, head, :],
                                attT_hi[:, head, cols].bitcast(F32).rearrange("p (b q) -> p b q", q=L), ALU.subtract)
                        last.then_inc(attT_lo_done, 1)
                if ahead:
                    low_q(t + 1, 1)
                    for half in range(2):
                        odd_values(t + 1, half)
                if attend:
                    wait(dve, sum_done, t)
                    wait(dve, ms2_done, t)
                    if isinstance(t, int) and t == 0:
                        dve.wait_ge(w_split, 5)
                    dve.wait_ge(x_res_done, t + 1)
                    for half in range(2):
                        dve.wait_ge(proj_mm, 2 * t + half + 1)
                        nc.vector.tensor_tensor(x1[:, 2 * half:2 * half + 2, :],
                                                ps[:, OUT + half, :].rearrange("p (k n) -> p k n", k=2),
                                                x_res[:, 2 * half:2 * half + 2, :], ALU.add).then_inc(x1_done, 1)
                if mlp and ahead:
                    silu(t - 1, CHUNKS - 2)
                    hidden(t - 1, CHUNKS - 2)
                if attend:
                    scale_rows(t, x1, inv2, inv2_done, x_scaled2, xT2_done, scaled2)

            over_tiles(dve, iteration)

        @block.tensor
        def _(pe):
            def three_passes(dst, a_hi, a_lo, b_hi, b_lo, first, last, skip=False):
                nc.tensor.matmul(dst, a_hi, b_hi, start=first, stop=False, skip_group_check=skip)
                nc.tensor.matmul(dst, a_hi, b_lo, start=False, stop=False, skip_group_check=skip)
                return nc.tensor.matmul(dst, a_lo, b_hi, start=False, stop=last, skip_group_check=skip)

            def transpose_norm1(u, c, bank):
                pe.wait_ge(scaled1, u + 1)
                for k in range(BLK):
                    last = nc.tensor.transpose(ps[:, bank, k * P:(k + 1) * P],
                                               x_scaled1[:, k, c * P:(c + 1) * P], ident)
                last.then_inc(xT1_done, 1)

            def transpose_norm2(u, c):
                pe.wait_ge(scaled2, u + 1)
                wait(pe, gained2, CH * u + c)
                for k in range(BLK):
                    last = nc.tensor.transpose(ps[:, EXTRA, k * P:(k + 1) * P],
                                               x_scaled2[:, k, c * P:(c + 1) * P], ident)
                last.then_inc(xT2_done, 1)

            def channel_major(m, c, dst):
                for i in range(CH):
                    w = slice(c * P, (c + 1) * P)
                    last = three_passes(dst, att_w_hi[:, m, i, w], att_w_lo[:, m, i, w],
                                        xn1_hi[:, i, :], xn1_lo[:, i, :], i == 0, i == CH - 1)
                return last

            def keep_clock_up(products):
                for n in range(products):
                    nc.tensor.matmul(ps[:, HIDDEN, :], att_w_hi[:, 0, 0, 0:P],
                                     att_w_hi[:, 1, :, :].rearrange("p c n -> p (c n)"), start=True, stop=True)

            def project_k(u):
                pe.wait_ge(xn1_lo_done, CH * u + CH)
                wait(pe, shift_done, PAIRS * u)
                wait(pe, exp_done, PAIRS * u)
                for c in range(CH):
                    channel_major(1, c, ps[:, SCORE + c, :]).then_inc(k_mm, 1)

            def project_q(u, c):
                wait(pe, h_done, CHUNKS * (u - 1) - LAG)
                channel_major(0, c, ps[:, GATE + c, :]).then_inc(q_mm, 1)

            def project_v(u, half):
                pe.wait_ge(k_lo_done, CH * u + half + 1)
                for k in (2 * half, 2 * half + 1):
                    tok = slice(k * P, (k + 1) * P)
                    for i in range(CH):
                        last = three_passes(ps[:, SCORE + k // 2, (k % 2) * D:(k % 2) * D + D],
                                            xn1_hi[:, i, tok], xn1_lo[:, i, tok],
                                            att_w_hi[:, 2, i, :], att_w_lo[:, 2, i, :], i == 0, i == CH - 1)
                last.then_inc(v_mm, 1)

            def scores(t, p):
                r, c = p // CH, p % CH
                if c == 0:
                    pe.wait_ge(stacked[r % 2], FILL * (2 * t + r // 2 + 1))
                if p == 0:
                    pe.wait_ge(v_even, 2 * t + 1)
                    pe.wait_ge(v_odd, 2 * t + 1)
                wait(pe, shift_done, PAIRS * t + p - (1 if alone(t) else 0))
                for b in range(SEQS):
                    tok = slice(b * L, (b + 1) * L)
                    last = nc.tensor.matmul(ps[:, score_bank(t, p), tok], q_stack[:, r % 2, c, b, :],
                                            k_stack[:, r % 2, c, tok], start=True, stop=True)
                last.then_inc(score_mm, 1)

            def transpose_shifted(t, p):
                pe.wait_ge(shift_done, PAIRS * t + p + 1)
                if p == 0:
                    pe.wait_ge(v_even, 2 * t + 2)
                    pe.wait_ge(v_odd, 2 * t + 2)
                wait(pe, exp_done, PAIRS * t + p)
                for k in range(BLK):
                    last = nc.tensor.transpose(ps[:, TRANS, k * P:(k + 1) * P], shifted[:, k * P:(k + 1) * P], ident)
                last.then_inc(shiftT_done, 1)

            def probs_values(t, p):
                pe.wait_ge(exp_done, PAIRS * t + p + 1)
                if p == 0:
                    wait(pe, x1_done, 2 * t)
                wait(pe, att_done, PAIRS * t + p)
                for k in range(BLK):
                    last = nc.tensor.matmul(ps[:, OUT, k * VW:(k + 1) * VW], probsT[:, p % 2, k * P:(k + 1) * P],
                                            values[:, k, pair_of(p), :], start=True, stop=True)
                last.then_inc(pv_mm, 1)

            def gate_hidden(u, j):
                wait(pe, h_done, CHUNKS * u + j)
                w = slice(j * P, (j + 1) * P)
                for bank, hi, lo, done in ((GATE, gate_w_hi, gate_w_lo, gate_mm), (HIDDEN, hid_w_hi, hid_w_lo, hid_mm)):
                    for i in range(CH):
                        if j == 0 and bank == GATE:
                            pe.wait_ge(xn2_hi_done, CH * u + i + 1)
                        nc.tensor.matmul(ps[:, bank, :], hi[:, i, w], xn2_hi[:, i, :], start=i == 0, stop=False)
                        nc.tensor.matmul(ps[:, bank, :], lo[:, i, w], xn2_hi[:, i, :], start=False, stop=False)
                    for i in range(CH):
                        if j == 0 and bank == GATE:
                            pe.wait_ge(xn2_lo_done, CH * u + i + 1)
                        last = nc.tensor.matmul(ps[:, bank, :], hi[:, i, w], xn2_lo[:, i, :], start=False,
                                                stop=i == CH - 1)
                    last.then_inc(done, 1)

            def down(u, j):
                pe.wait_ge(h_lo_done, CHUNKS * u + j + 1)
                if j == 0:
                    wait(pe, result_done, 2 * u)
                for k in range(BLK):
                    tok = slice(k * P, (k + 1) * P)
                    last = three_passes(ps[:, Y + k // 2, (k % 2) * D:(k % 2) * D + D],
                                        h_hi[:, j % 2, tok], h_lo[:, j % 2, tok],
                                        out_w_hi[:, j, :], out_w_lo[:, j, :],
                                        j == 0 and k % 2 == 0, j == CHUNKS - 1, skip=True)
                last.then_inc(down_mm, 1)

            def gains_and_shifts(norm):
                for m in (2 * norm, 2 * norm + 1):
                    for c in range(CH):
                        at = ((m % 2) * CH + c) * B
                        nc.tensor.matmul(ps[:, Y + norm, at:at + B], mod_w[:, m, c * P:(c + 1) * P], cond_sb[:, :],
                                         start=True, stop=True).then_inc(mod_mm, 1)

            pe.wait_ge(mod_in, 2 * 16)
            gains_and_shifts(0)
            pe.wait_ge(consts_in, 16)
            for c in range(CH):
                transpose_norm1(0, c, SCORE + c)
            gains_and_shifts(1)
            pe.wait_ge(w_hi_done, 1)
            keep_clock_up(FILL_K)
            pe.wait_ge(w_split, 1)
            project_k(0)
            for c in range(CH):
                project_q(0, c)
            pe.wait_ge(w_split, 2)
            for half in range(2):
                project_v(0, half)

            def iteration(t, attend, mlp, finish, ahead):
                for p in range(PAIRS):
                    if alone(t) and p == 0:
                        pe.wait_ge(q_lo_done, CH)
                        keep_clock_up(FILL_S0)
                        scores(t, 0)
                    if not alone(t) and attend:
                        if isinstance(t, int) and t == 1 and p == 0:
                            pe.wait_ge(q_lo_done, 2 * CH)
                            keep_clock_up(FILL_S1)
                        scores(t, p)
                        if isinstance(t, int) and t == 1 and p < LAG:
                            keep_clock_up(FILL_STEP)
                    if alone(t) and p + 1 < PAIRS:
                        scores(t, p + 1)
                        keep_clock_up(FILL_STEP)
                    if finish and not attend and p == 0:
                        gate_hidden(t - 2, CHUNKS - 1)
                    if mlp and p < CH:
                        transpose_norm2(t - 1, p)
                    if ahead and p == step_ahead(t, 6):
                        transpose_norm1(t + 1, 0, EXTRA)
                    if finish and attend and p == 0:
                        gate_hidden(t - 2, CHUNKS - 1)
                    if finish and p == 1:
                        down(t - 2, CHUNKS - 2)
                    if finish and attend and p == 2:
                        down(t - 2, CHUNKS - 1)
                    if attend and 1 <= p <= LAG:
                        probs_values(t, p - 1)
                    if mlp and p >= LAG:
                        if isinstance(t, int) and t == 1 and p == LAG:
                            pe.wait_ge(w_split, 5)
                        gate_hidden(t - 1, p - LAG)
                    if finish and not attend and p == 2:
                        down(t - 2, CHUNKS - 1)
                    if attend:
                        transpose_shifted(t, p)
                    if mlp and p > LAG:
                        down(t - 1, p - LAG - 1)
                    if attend and p > LAG:
                        probs_values(t, p - 1)
                    if ahead and p == step_ahead(t, 6):
                        pe.wait_ge(gained1, CH * t + CH + 1)
                        transpose_norm1(t + 1, 1, EXTRA)
                if ahead:
                    project_k(t + 1)
                if mlp and not ahead:
                    gate_hidden(t - 1, CHUNKS - 2)
                if attend:
                    probs_values(t, PAIRS - 1)
                if ahead:
                    project_q(t + 1, 0)
                if attend:
                    pe.wait_ge(att_done, PAIRS * t + PAIRS)
                    if ahead:
                        pe.wait_ge(gained1, CH * t + 2 * CH)
                    for half in range(2):
                        for b in range(SEQS // 2):
                            last = nc.tensor.transpose(
                                ps[:, OUT + half, b * P:(b + 1) * P],
                                att[:, half * 4 + b, :, :].rearrange("p n d -> p (n d)"), ident)
                        last.then_inc(attT_mm, 1)
                if mlp and not ahead:
                    down(t - 1, CHUNKS - 3)
                if ahead:
                    project_q(t + 1, 1)
                    for half in range(2):
                        project_v(t + 1, half)
                if attend:
                    for k in range(BLK):
                        tok = slice(k * P, (k + 1) * P)
                        pe.wait_ge(attT_lo_done, 2 * t + k // 2 + 1)
                        for head in range(2):
                            last = three_passes(ps[:, OUT + k // 2, (k % 2) * D:(k % 2) * D + D],
                                                attT_hi[:, head, tok], attT_lo[:, head, tok],
                                                att_w_hi[:, 3, head, :], att_w_lo[:, 3, head, :], head == 0, head == 1)
                        if k % 2:
                            last.then_inc(proj_mm, 1)
                if mlp and ahead:
                    pe.wait_ge(q_lo_done, CH * t + 2 * CH)
                    gate_hidden(t - 1, CHUNKS - 2)
                    down(t - 1, CHUNKS - 3)

            over_tiles(pe, iteration)


_NAMES = ["x", "condT", "modT", "attT", "gateT", "hidT", "outT", "consts"]


def kernel(**inputs):
    import numpy as np
    import concourse.bacc as bacc
    from concourse.bass_utils import run_bass_kernel_spmd

    a = {k.removeprefix("L0_cond_"): np.asarray(v) for k, v in inputs.items()}
    wo_rows = a["Wo"].T.reshape(PAIRS, 2, DH, D).transpose(1, 0, 2, 3).reshape(D, D)
    att = np.stack([a["Wq"].T, a["Wk"].T, a["Wv"].T, wo_rows]).reshape(4, CH, P, D).transpose(2, 0, 1, 3)
    modulations = ("g1", "b1", "g2", "b2")
    biases = np.concatenate([a[m + "b"].reshape(CH, P).T for m in modulations], 1)
    head_of_row = (np.arange(P) // DH) % 2
    shape_consts = np.concatenate([np.eye(P), np.stack([(head_of_row == n) * 0.25 for n in range(2)], 1)], 1)
    laid = {
        "x": a["x"], "condT": a["cond_256"].T, "modT": np.stack([a[m + "w"].T for m in modulations], 1),
        "attT": att.reshape(P, 4 * CH * D), "gateT": a["gate_w"].T, "hidT": a["hid_w"].T, "outT": a["out_w"].T,
        "consts": np.concatenate([shape_consts.astype(np.float32), biases], 1),
    }
    nc = bacc.Bacc("TRN2", target_bir_lowering=False, num_devices=1)
    arrays, args = {}, []
    for name in _NAMES:
        v = np.ascontiguousarray(laid[name])
        arrays[f"in_{name}"] = v
        args.append(nc.dram_tensor(f"in_{name}", v.shape, mybir.dt.from_np(v.dtype), kind="ExternalInput").ap())
    args.append(nc.dram_tensor("out_0", (B, L, D), F32, kind="ExternalOutput").ap())
    conditioned_block(nc, *args)
    r = run_bass_kernel_spmd(nc, [arrays], core_ids=[0])
    return r.results[0]["out_0"]
```
